# Optimizing a Trainium2 kernel written in Bass

```python
import numpy as np
import jax
import jax.numpy as jnp

def _softmax(x, axis=-1):
    return jax.nn.softmax(x, axis=axis)

def _gelu(x):
    return jax.nn.gelu(x, approximate=True)

def _silu(x):
    return jax.nn.silu(x)

def _sigmoid(x):
    return jax.nn.sigmoid(x)

def _layernorm(x, axis=-1, eps=1e-05):
    m = jnp.mean(x, axis=axis, keepdims=True)
    v = jnp.var(x, axis=axis, keepdims=True)
    return (x - m) / jnp.sqrt(v + eps)

def _scatter_add(tgt, idx, src, axis=0):
    return tgt.at[idx].add(src)

def _segment_sum(src, seg, n):
    return jax.ops.segment_sum(src, seg, n)
kernel_name = 'mk_prb_d1_jaxref_r4_7d74be'

def setup_inputs(seed: int=0):
    np.random.seed(seed)
    _w = jnp.asarray

    def _L0_attn_setup():
        import jax, jax.numpy as jnp
        import numpy as np
        import math
        D_MODEL, D_STATE, D_CONV = (256, 16, 4)
        D_INNER = 2 * D_MODEL
        DT_RANK = math.ceil(D_MODEL / 16)
        B, L = (4, 512)

        def _layernorm(x, g, b, eps=1e-05):
            m = jnp.mean(x, axis=-1, keepdims=True)
            v = jnp.mean(jnp.square(x - m), axis=-1, keepdims=True)
            return (x - m) * jax.lax.rsqrt(v + eps) * g + b

        def _mamba(xn, W_in, conv_w, conv_b, W_xp, W_dt, dt_bias, A_log, D_skip, W_out):
            xz = xn @ W_in
            xi, z = jnp.split(xz, 2, axis=-1)
            xi_t = jnp.transpose(xi, (0, 2, 1))
            xc = jax.lax.conv_general_dilated(xi_t, conv_w, window_strides=(1,), padding=[(D_CONV - 1, 0)], feature_group_count=D_INNER, dimension_numbers=('NCH', 'OIH', 'NCH'))
            xc = jnp.transpose(xc, (0, 2, 1)) + conv_b
            xc = jax.nn.silu(xc)
            x_dbl = xc @ W_xp
            dt_lo, Bm, Cm = jnp.split(x_dbl, [DT_RANK, DT_RANK + D_STATE], axis=-1)
            delta = jax.nn.softplus(dt_lo @ W_dt + dt_bias)
            A = -jnp.exp(A_log)

            def step(h, inp):
                dt_t, B_t, C_t, u_t = inp
                dA = jnp.exp(dt_t[..., None] * A)
                h = h * dA + (dt_t * u_t)[..., None] * B_t[:, None, :]
                y = jnp.einsum('bdn,bn->bd', h, C_t)
                return (h, y)
            h0 = jnp.zeros((xn.shape[0], D_INNER, D_STATE), xn.dtype)
            inputs = (jnp.transpose(delta, (1, 0, 2)), jnp.transpose(Bm, (1, 0, 2)), jnp.transpose(Cm, (1, 0, 2)), jnp.transpose(xc, (1, 0, 2)))
            _, ys = jax.lax.scan(step, h0, inputs)
            y = jnp.transpose(ys, (1, 0, 2)) + xc * D_skip
            y = y * jax.nn.silu(z)
            return y @ W_out
        key = jax.random.key(seed)
        ks = jax.random.split(key, 10)
        s = 0.02
        x = jax.random.normal(ks[0], (B, L, D_MODEL), dtype=jnp.float32)
        ln_g = jnp.ones((D_MODEL,), jnp.float32)
        ln_b = jnp.zeros((D_MODEL,), jnp.float32)
        W_in = jax.random.normal(ks[1], (D_MODEL, 2 * D_INNER), jnp.float32) * s
        conv_w = jax.random.normal(ks[2], (D_INNER, 1, D_CONV), jnp.float32) * s
        conv_b = jnp.zeros((D_INNER,), jnp.float32)
        W_xp = jax.random.normal(ks[3], (D_INNER, DT_RANK + 2 * D_STATE), jnp.float32) * s
        W_dt = jax.random.normal(ks[4], (DT_RANK, D_INNER), jnp.float32) * DT_RANK ** (-0.5)
        dt_bias = jnp.full((D_INNER,), float(np.log(np.expm1(0.01))), jnp.float32)
        A_log = jnp.log(jnp.broadcast_to(jnp.arange(1, D_STATE + 1, dtype=jnp.float32), (D_INNER, D_STATE)))
        D_skip = jnp.ones((D_INNER,), jnp.float32)
        W_out = jax.random.normal(ks[5], (D_INNER, D_MODEL), jnp.float32) * s
        return dict(x=x, ln_g=ln_g, ln_b=ln_b, W_in=W_in, conv_w=conv_w, conv_b=conv_b, W_xp=W_xp, W_dt=W_dt, dt_bias=dt_bias, A_log=A_log, D_skip=D_skip, W_out=W_out)
    _L0_attn_in = _L0_attn_setup()

    def _L0_ffn_setup():
        import jax, jax.numpy as jnp
        import numpy as np
        DIM = 256
        HIDDEN = 768
        SCALE = 1.0 / 127.0

        def _dequant(w_int, dtype):
            return w_int.astype(dtype) * jnp.asarray(SCALE, dtype)
        key = jax.random.key(seed)
        k_x, k_g, k_u, k_d = jax.random.split(key, 4)
        x = jax.random.normal(k_x, (4, 512, DIM), dtype=jnp.float32)
        w_gate = jax.random.randint(k_g, (HIDDEN, DIM), -127, 128, dtype=jnp.int32)
        w_up = jax.random.randint(k_u, (HIDDEN, DIM), -127, 128, dtype=jnp.int32)
        w_down = jax.random.randint(k_d, (DIM, HIDDEN), -127, 128, dtype=jnp.int32)
        return {'x': x, 'w_gate': w_gate, 'w_up': w_up, 'w_down': w_down}
    _L0_ffn_in = _L0_ffn_setup()
    _d = {'L0_attn_x': _L0_attn_in['x'], 'L0_attn_ln_g': _L0_attn_in['ln_g'], 'L0_attn_ln_b': _L0_attn_in['ln_b'], 'L0_attn_W_in': _L0_attn_in['W_in'], 'L0_attn_conv_w': _L0_attn_in['conv_w'], 'L0_attn_conv_b': _L0_attn_in['conv_b'], 'L0_attn_W_xp': _L0_attn_in['W_xp'], 'L0_attn_W_dt': _L0_attn_in['W_dt'], 'L0_attn_dt_bias': _L0_attn_in['dt_bias'], 'L0_attn_A_log': _L0_attn_in['A_log'], 'L0_attn_D_skip': _L0_attn_in['D_skip'], 'L0_attn_W_out': _L0_attn_in['W_out'], 'L0_ffn_w_gate': _L0_ffn_in['w_gate'], 'L0_ffn_w_up': _L0_ffn_in['w_up'], 'L0_ffn_w_down': _L0_ffn_in['w_down']}
    _x0 = _d['L0_attn_x']
    _d['L0_attn_x'] = jax.random.normal(jax.random.fold_in(jax.random.key(seed), 1), (32, 512, 256), dtype=_x0.dtype)
    del _x0
    return _d

def reference(L0_attn_x, L0_attn_ln_g, L0_attn_ln_b, L0_attn_W_in, L0_attn_conv_w, L0_attn_conv_b, L0_attn_W_xp, L0_attn_W_dt, L0_attn_dt_bias, L0_attn_A_log, L0_attn_D_skip, L0_attn_W_out, L0_ffn_w_gate, L0_ffn_w_up, L0_ffn_w_down):

    def _L0_attn_ref(x, ln_g, ln_b, W_in, conv_w, conv_b, W_xp, W_dt, dt_bias, A_log, D_skip, W_out):
        import jax, jax.numpy as jnp
        import numpy as np
        import math
        D_MODEL, D_STATE, D_CONV = (256, 16, 4)
        D_INNER = 2 * D_MODEL
        DT_RANK = math.ceil(D_MODEL / 16)
        B, L = (4, 512)

        def _layernorm(x, g, b, eps=1e-05):
            m = jnp.mean(x, axis=-1, keepdims=True)
            v = jnp.mean(jnp.square(x - m), axis=-1, keepdims=True)
            return (x - m) * jax.lax.rsqrt(v + eps) * g + b

        def _mamba(xn, W_in, conv_w, conv_b, W_xp, W_dt, dt_bias, A_log, D_skip, W_out):
            xz = xn @ W_in
            xi, z = jnp.split(xz, 2, axis=-1)
            xi_t = jnp.transpose(xi, (0, 2, 1))
            xc = jax.lax.conv_general_dilated(xi_t, conv_w, window_strides=(1,), padding=[(D_CONV - 1, 0)], feature_group_count=D_INNER, dimension_numbers=('NCH', 'OIH', 'NCH'))
            xc = jnp.transpose(xc, (0, 2, 1)) + conv_b
            xc = jax.nn.silu(xc)
            x_dbl = xc @ W_xp
            dt_lo, Bm, Cm = jnp.split(x_dbl, [DT_RANK, DT_RANK + D_STATE], axis=-1)
            delta = jax.nn.softplus(dt_lo @ W_dt + dt_bias)
            A = -jnp.exp(A_log)

            def step(h, inp):
                dt_t, B_t, C_t, u_t = inp
                dA = jnp.exp(dt_t[..., None] * A)
                h = h * dA + (dt_t * u_t)[..., None] * B_t[:, None, :]
                y = jnp.einsum('bdn,bn->bd', h, C_t)
                return (h, y)
            h0 = jnp.zeros((xn.shape[0], D_INNER, D_STATE), xn.dtype)
            inputs = (jnp.transpose(delta, (1, 0, 2)), jnp.transpose(Bm, (1, 0, 2)), jnp.transpose(Cm, (1, 0, 2)), jnp.transpose(xc, (1, 0, 2)))
            _, ys = jax.lax.scan(step, h0, inputs)
            y = jnp.transpose(ys, (1, 0, 2)) + xc * D_skip
            y = y * jax.nn.silu(z)
            return y @ W_out
        xn = _layernorm(x, ln_g, ln_b)
        return _mamba(xn, W_in, conv_w, conv_b, W_xp, W_dt, dt_bias, A_log, D_skip, W_out) + x

    def _L0_ffn_ref(x, w_gate, w_up, w_down):
        import jax, jax.numpy as jnp
        import numpy as np
        DIM = 256
        HIDDEN = 768
        SCALE = 1.0 / 127.0

        def _dequant(w_int, dtype):
            return w_int.astype(dtype) * jnp.asarray(SCALE, dtype)
        wg = _dequant(w_gate, x.dtype)
        wu = _dequant(w_up, x.dtype)
        wd = _dequant(w_down, x.dtype)
        gate = jnp.einsum('bsd,hd->bsh', x, wg)
        up = jnp.einsum('bsd,hd->bsh', x, wu)
        h = jax.nn.silu(gate) * up
        return jnp.einsum('bsh,dh->bsd', h, wd)
    x = L0_attn_x
    xn = _layernorm(x, axis=-1)
    x = x + _L0_attn_ref(xn, L0_attn_ln_g, L0_attn_ln_b, L0_attn_W_in, L0_attn_conv_w, L0_attn_conv_b, L0_attn_W_xp, L0_attn_W_dt, L0_attn_dt_bias, L0_attn_A_log, L0_attn_D_skip, L0_attn_W_out) + _L0_ffn_ref(xn, L0_ffn_w_gate, L0_ffn_w_up, L0_ffn_w_down)
    return x

_drawn_inputs = setup_inputs


def setup_inputs(seed=0):
    import zlib

    import numpy as np

    out = dict(_drawn_inputs(seed))
    spreads = {'L0_attn_ln_g': (1.0, 0.6),
     'L0_attn_ln_b': (0.0, 0.8),
     'L0_attn_conv_b': (0.0, 0.8),
     'L0_attn_dt_bias': (-4.600165843963623, 0.6),
     'L0_attn_D_skip': (1.0, 0.6)}
    factors = {'L0_attn_W_in': 8.0,
     'L0_attn_conv_w': 8.0,
     'L0_attn_W_xp': 8.0,
     'L0_attn_W_dt': 8.0,
     'L0_attn_A_log': 8.0,
     'L0_attn_W_out': 8.0}
    for name, (base, spread) in spreads.items():
        noise = np.random.default_rng([zlib.crc32(name.encode()), seed]).standard_normal(out[name].shape)
        drawn = base * np.exp(spread * noise) if base else spread * noise
        out[name] = jnp.asarray(drawn.astype(out[name].dtype))
    for name, factor in factors.items():
        out[name] = (out[name] * factor).astype(out[name].dtype)
    return out
```

```python
from contextlib import ExitStack

import concourse.bass as bass
from concourse import mybir

ALU = mybir.AluOpType
ACT = mybir.ActivationFunctionType
F32 = mybir.dt.float32
BF16 = mybir.dt.bfloat16
I32 = mybir.dt.int32

P = 128
EPS = 1e-5
QUANT = 1.0 / 127.0
SMALL = 0.02
THIRD_ROOT = 3.0 ** -0.5
TABLES = "natural_log_exp_and_others"

SLOT_FILLS = {
    0: [("SPREAD", 4)], 1: [("SPREAD", 5)], 2: [("SPREAD", 6)], 3: [("SPREAD", 7), ("TURN", 3)],
    4: [("DT", 3)], 5: [("OUT", 0)], 6: [("OUT", 1), ("LN", 0), ("LN", 1)], 9: [("LN2", 0), ("LN2", 1)],
    10: [("GATE", 0), ("GATE", 1)], 11: [("GATE", 2), ("TURN", 0)], 12: [("GATE", 3), ("XI", 0)],
    13: [("GATE", 4)], 14: [("GATE", 5)], 15: [("XI", 1)], 16: [("XI", 2), ("Z", 0)],
    17: [("XI", 3)], 18: [("UP", 0), ("Z", 2)], 19: [("UP", 1), ("TURN", 1)], 20: [("UP", 2), ("Z", 3), ("Z", 1)],
    21: [("UP", 3)], 22: [("UP", 4)], 23: [("UP", 5), ("XP", 0)], 24: [("DOWN", 0)],
    25: [("DT", 0)], 26: [("DT", 1), ("DT", 2)], 27: [("DOWN", 1), ("TURN", 2)],
    28: [("SPREAD", 0)], 29: [("SPREAD", 1)], 30: [("SPREAD", 2)], 31: [("SPREAD", 3)],
}
ACT_SLOTS = {
    0: [("SPREAD", 0)], 1: [("SPREAD", 1), ("XC3", 0)], 2: [("SPREAD", 2)], 3: [("SPREAD", 3)],
    4: [("SPREAD", 4)], 5: [("SPREAD", 5)], 6: [("SPREAD", 6)], 7: [("SPREAD", 7), ("TURN", 3), ("ZCOPY", 0)],
    9: [("DT", 3)], 10: [("LN", 0), ("LN", 1)], 13: [("LN2", 0), ("LN2", 1)],
    14: [("GATE", 0)], 15: [("GATE", 1), ("GATE", 2), ("TURN", 0)], 16: [("GATE", 3), ("XI", 0)],
    17: [("GATE", 4)], 18: [("GATE", 5), ("FFNSILU", 0), ("XI", 1)], 20: [("XI", 2), ("Z", 0)], 21: [("XI", 3)],
    22: [("Z", 2), ("TURN", 1)], 24: [("Z", 3), ("Z", 1), ("SILU", 0)],
    27: [("XP", 0)], 28: [("MID", 0)], 29: [("LOW", 0), ("DT", 0)], 30: [("DT", 1)],
    31: [("DT", 2), ("TURN", 2)],
}
DVE_SLOTS = {
    1: [("STATS", 0)], 2: [("YGATE", 3)], 4: [("XN", 0)], 6: [("OUT", 0)], 7: [("OUT", 1)], 8: [("XN2", 0), ("DT", 3)],
    10: [("YGATE", 0)], 14: [("XI", 0)], 16: [("XI", 1)], 18: [("XI", 2), ("YGATE", 1), ("UP", 0)],
    19: [("XI", 3)], 20: [("UP", 1)], 21: [("UP", 2)], 22: [("UP", 3)], 23: [("UP", 4)],
    24: [("XP", 0), ("UP", 5)], 25: [("DOWN", 0), ("LOW", 0)],
    26: [("YGATE", 2), ("DT", 0)], 27: [("DT", 1)], 28: [("DOWN", 1), ("DT", 2)],
}
POOL_SLOTS = {1: [("RSTD", 0)], 4: [("RSTD", 1)], 5: [("SUM", 0)]}


def bass_mamba_ffn_block_kernel(
    nc: bass.Bass, x: bass.AP, ln_g: bass.AP, ln_b: bass.AP, w_in: bass.AP, conv_w: bass.AP,
    conv_b: bass.AP, w_xp: bass.AP, w_dt: bass.AP, dt_bias: bass.AP, a_log: bass.AP, d_skip: bass.AP,
    w_out: bass.AP, w_gate: bass.AP, w_up: bass.AP, w_down: bass.AP, ident: bass.AP, pick: bass.AP,
    out: bass.AP,
):
    NB, L, D = x.shape
    DI = w_out.shape[0]
    N = a_log.shape[-1]
    R = w_dt.shape[0]
    K = conv_w.shape[-1]
    HID = w_gate.shape[-1]
    TT, KD, CT, HT = L // P, D // P, DI // P, HID // P
    PAIRS = N // 2
    STEPS = CT * PAIRS
    RING = 4
    AHEAD = 4
    assert L == 512 and 3 * 2 * N + R <= P and STEPS % RING == 0

    order = []
    for s in range(STEPS):
        for name, i in SLOT_FILLS.get(s, []):
            order += [("SPREAD", 4 * i + j) for j in range(4)] if name == "SPREAD" else [(name, i)]
    stage_names = ("LN", "LN2", "GATE", "XI", "Z", "UP", "XP", "DOWN", "DT", "SPREAD")
    def opening(name, i):
        return name in stage_names and (name, i) != ("DT", CT - 1) and not (name == "SPREAD" and i >= 4 * AHEAD)
    first_order = [f for f in order if opening(*f)]
    closing_order = [("TURN", CT - 1), ("OUT", 0), ("OUT", 1)]
    def places(fills, last_bank):
        banks = [(last_bank - (len(fills) - 1 - n)) % 2 for n in range(len(fills))]
        at, used = {}, [0, 0]
        for f, bank in zip(fills, banks):
            used[bank] += 1
            at[f] = (bank, used[bank])
        return at, used
    in_pass, per_pass = places(order, 0)
    in_first, per_first = places(first_order, 0)
    in_closing, _ = places(closing_order, 0)

    ctx = ExitStack()
    with ctx:
        def sb(name, shape, dt=F32):
            return ctx.enter_context(nc.sbuf_tensor(name, shape, dt))

        def ps(name, shape):
            return ctx.enter_context(nc.psum_tensor(name, shape, F32))

        def sem(name):
            return ctx.enter_context(nc.semaphore(name))

        W_in = sb("W_in", [P, KD, 2 * DI])
        W_out = sb("W_out", [P, CT, D])
        W_g = sb("W_g", [P, KD, HID])
        W_u = sb("W_u", [P, KD, HID])
        W_d = sb("W_d", [P, HT, D])
        W_x = sb("W_x", [P, CT, 3 * 2 * N + R])
        W_t = sb("W_t", [R, DI])
        eye = sb("eye", [P, P])
        choose = sb("choose", [3 * 2 * N, 2 * N], BF16)
        gain = sb("gain", [P, KD])
        shift = sb("shift", [P, KD])
        taps = sb("taps", [P, CT, K])
        conv_bias = sb("conv_bias", [P, CT])
        step_bias = sb("step_bias", [P, CT])
        skip = sb("skip", [P, CT])
        negA = sb("negA", [P, CT, N])
        pick_in = sb("pick_in", [3 * 2 * N, 2 * N])
        c_eps = sb("c_eps", [P, 2 * TT])
        spare = sb("spare", [P, 4])
        c_bias = sb("c_bias", [P, 3])

        X = sb("X", [P, TT, D])
        XN = sb("XN", [P, TT, D])
        XNT = sb("XNT", [P, KD, L])
        XHT = sb("XHT", [P, KD, L])
        stats = sb("stats", [P, TT, 6])
        moments = sb("moments", [P, TT, 2])
        rstd = sb("rstd", [P, 2, TT])
        HG = sb("HG", [P, HT, L])
        RES = sb("RES", [P, TT, D])
        CPRE = sb("CPRE", [P, CT, L])
        XC = sb("XC", [P, CT, L])
        DELTA = sb("DELTA", [P, CT, L])
        Z = sb("Z", [P, CT, TT * P])
        pieces = sb("pieces", [3 * 2 * N, L], BF16)
        Bs = sb("Bs", [P, N, L])
        Cs = sb("Cs", [P, N, L])
        YGT = sb("YGT", [P, CT, L])

        decay = sb("decay", [P, RING, 2, L])
        h = sb("h", [P, RING, 2, L])
        turnbuf = sb("turnbuf", [P, L])

        Zlate = XN[:, :, :].rearrange("p a b -> p (a b)").rearrange("p (c f) -> p c f", c=2)
        rest = XNT[:, 0, :]
        dt_in = XNT[0:R, 1, :]
        mid_low = XNT[64:64 + 2 * N, 1, 0:L // 2].bitcast(BF16)
        t_e, t_l, t_u = CPRE[:, 0, :], CPRE[:, 1, :], CPRE[:, 2, :]
        late_u = CPRE[:, CT - 1, :]

        general = [ps("general0", [P, L]), ps("general1", [P, L])]
        yT = ps("yT", [P, TT * P])
        du = ps("du", [P, 1, L])
        drive = ps("drive", [P, 2, 2, L])

        filled = [sem("filled0"), sem("filled1")]
        drained = [sem("drained0"), sem("drained1")]
        weights_in = sem("weights_in")
        ints_in = sem("ints_in")
        ints_made = sem("ints_made")
        a_made = sem("a_made")
        x_in = sem("x_in")
        consts_made = sem("consts_made")
        stats_seen = sem("stats_seen")
        moments_made = sem("moments_made")
        pow_step = sem("pow_step")
        rstd_made = sem("rstd_made")
        xn_made = sem("xn_made")
        xh_made = sem("xh_made")
        sum_made = sem("sum_made")
        silu_gate_made = sem("silu_gate_made")
        conv_step = sem("conv_step")
        conv_scaled = sem("conv_scaled")
        u_made = sem("u_made")
        u_moved = sem("u_moved")
        z_silu_made = sem("z_silu_made")
        z_made = sem("z_made")
        high_made = sem("high_made")
        mid_made = sem("mid_made")
        rest_made = sem("rest_made")
        pieces_made = sem("pieces_made")
        softplus_step = sem("softplus_step")
        softplus_parts = sem("softplus_parts")
        delta_step = sem("delta_step")
        delta_made = sem("delta_made")
        du_made = sem("du_made")
        skip_made = sem("skip_made")
        decay_made = sem("decay_made")
        drive_made = sem("drive_made")
        scanned = sem("scanned")
        weighted = sem("weighted")
        summed = sem("summed")
        gated = sem("gated")
        spilled = sem("spilled")
        reloaded = sem("reloaded")
        stored = sem("stored")

        x_v = x.rearrange("b (t p) d -> b p t d", p=P)
        out_v = out.rearrange("b (t p) d -> b p t d", p=P)

        def at_fill(when, name, i):
            b, late = when
            if b is None:
                return in_first[name, i]
            if isinstance(b, str):
                bank, n = in_closing[name, i]
                return bank, per_first[bank] + NB * per_pass[bank] + n
            bank, n = in_pass[name, i]
            base = per_first[bank] + n - (per_pass[bank] if late else 0)
            assert base > 0 and (not late or in_first[name, i] == (bank, base))
            return bank, per_pass[bank] * b + base

        def wait_filled(eng, when, name, i):
            bank, n = at_fill(when, name, i)
            eng.wait_ge(filled[bank], n)
            return general[bank], drained[bank]

        def wait_drained(eng, when, name, i):
            bank, n = at_fill(when, name, i)
            eng.wait_ge(drained[bank], n)

        def wait_all_drained(eng, when, name, which):
            latest = {}
            for i in which:
                bank, n = (in_closing if isinstance(when[0], str) else in_pass)[name, i]
                if bank not in latest or n > latest[bank][0]:
                    latest[bank] = (n, i)
            for n, i in latest.values():
                wait_drained(eng, when, name, i)

        block = ctx.enter_context(nc.Block())

        @block.sync
        def _(sp):
            sp.dma_start(HG[:, 0:3, :].bitcast(I32).rearrange("p a b -> p (a b)").rearrange("p (k n) -> p k n", k=KD),
                         w_gate.rearrange("(k p) n -> p k n", p=P)).then_inc(ints_in, 16)
            sp.dma_start(HG[:, 3:6, :].bitcast(I32).rearrange("p a b -> p (a b)").rearrange("p (k n) -> p k n", k=KD),
                         w_up.rearrange("(k p) n -> p k n", p=P)).then_inc(ints_in, 16)
            sp.dma_start(CPRE[:, 0:3, :].bitcast(I32).rearrange("p a b -> p (a b)").rearrange("p (k n) -> p k n", k=HT),
                         w_down.rearrange("(k p) n -> p k n", p=P)).then_inc(ints_in, 16)
            sp.dma_start(X[:, :, :], x_v[0]).then_inc(x_in, 16)
            sp.dma_start(eye[:, :], ident).then_inc(weights_in, 16)
            sp.dma_start(W_in[:, :, :], w_in.rearrange("(k p) n -> p k n", p=P)).then_inc(weights_in, 16)
            sp.dma_start(W_out[:, :, :], w_out.rearrange("(k p) n -> p k n", p=P)).then_inc(weights_in, 16)
            sp.dma_start(W_x[:, :, :], w_xp.rearrange("(k p) n -> p k n", p=P)).then_inc(weights_in, 16)
            sp.dma_start(W_t[:, :], w_dt).then_inc(weights_in, 16)
            sp.dma_start(pick_in[:, :], pick).then_inc(weights_in, 16)
            for tile, vector in ((gain, ln_g), (shift, ln_b), (conv_bias, conv_b), (step_bias, dt_bias), (skip, d_skip)):
                sp.dma_start(tile[:, :], vector).then_inc(weights_in, 16)
            sp.dma_start(taps[:, :, :], conv_w).then_inc(weights_in, 16)
            sp.dma_start(negA[:, :, :], a_log).then_inc(weights_in, 16)

            def spill(when, row):
                wait_all_drained(sp, when, "DOWN", range(2))
                sp.dma_start(out_v[row], RES[:, :, :]).then_inc(spilled, 16)

            def load_x(row):
                sp.dma_start(X[:, :, :], x_v[row]).then_inc(x_in, 16)

            def finish(when, b, row):
                sp.wait_ge(spilled, 16 * b)
                sp.dma_start(RES[:, :, :], out_v[row]).then_inc(reloaded, 16)
                wait_all_drained(sp, when, "OUT", range(2))
                sp.dma_start(out_v[row], RES[:, :, :]).then_inc(stored, 16)

            spill((None, 0), 0)
            load_x(1)
            spill((0, 0), 1)
            load_x(2)
            with sp.Fori(1, NB - 2) as b:
                finish((b, 0), b + 1, b - 1)
                spill((b, 0), b + 1)
                load_x(b + 2)
            finish((NB - 2, 0), NB - 1, NB - 3)
            spill((NB - 2, 0), NB - 1)
            load_x(NB - 1)
            finish((NB - 1, 0), NB, NB - 2)
            wait_all_drained(sp, (NB - 1, 0), "DOWN", range(2))
            finish(("end", 0), NB, NB - 1)
            sp.wait_ge(stored, 16 * (NB + 1))

        @block.tensor
        def _(pe):
            def open_bank(when, name, i):
                bank, n = at_fill(when, name, i)
                if not (when[0] is None and n == 1):
                    pe.wait_ge(drained[bank], n - 1)
                return general[bank], filled[bank]

            def turned(when, name, i, k):
                pe.wait_ge(xn_made if name == "LN" else xh_made, k + 1)
                bank, done = open_bank(when, name, i)
                for t in range(TT):
                    last = pe.transpose(bank[:, t * P:(t + 1) * P], XN[:, t, i * P:(i + 1) * P], eye[:, :])
                last.then_inc(done, 1)

            def product(when, name, i, weight, moving, tiles):
                bank, done = open_bank(when, name, i)
                for c in range(tiles):
                    w = weight(c)
                    last = pe.matmul(bank[0:w.shape[-1], :], w, moving(c), start=(c == 0), stop=(c == tiles - 1))
                last.then_inc(done, 1)

            def stage(when, name, i, k):
                if name in ("LN", "LN2"):
                    turned(when, name, i, k)
                elif name == "GATE":
                    if i == 0:
                        wait_all_drained(pe, when, "LN", range(KD))
                    product(when, name, i, lambda c: W_g[:, c, i * P:(i + 1) * P], lambda c: XNT[:, c, :], KD)
                elif name == "UP":
                    product(when, name, i, lambda c: W_u[:, c, i * P:(i + 1) * P], lambda c: XNT[:, c, :], KD)
                elif name == "XI":
                    if i == 0:
                        wait_all_drained(pe, when, "LN2", range(KD))
                    product(when, name, i, lambda c: W_in[:, c, i * P:(i + 1) * P], lambda c: XHT[:, c, :], KD)
                elif name == "Z":
                    bank, done = open_bank(when, name, i)
                    for t in range(TT):
                        for c in range(KD):
                            last = pe.matmul(bank[:, t * P:(t + 1) * P], XHT[:, c, t * P:(t + 1) * P],
                                             W_in[:, c, DI + i * P:DI + (i + 1) * P],
                                             start=(c == 0), stop=(c == KD - 1))
                    last.then_inc(done, 1)
                elif name == "XP":
                    pe.wait_ge(u_made, k + 1)
                    product(when, name, 0, lambda c: W_x[:, c, :],
                            lambda c: late_u if c == CT - 1 else XC[:, c, :], CT)
                elif name == "DOWN":
                    wait_all_drained(pe, when, "UP", range(HT))
                    bank, done = open_bank(when, name, i)
                    for t in range(2):
                        for c in range(HT):
                            last = pe.matmul(bank[:, t * D:(t + 1) * D], HG[:, c, (2 * i + t) * P:(2 * i + t + 1) * P],
                                             W_d[:, c, :], start=(c == 0), stop=(c == HT - 1))
                    last.then_inc(done, 1)
                elif name == "DT":
                    pe.wait_ge(high_made, k + 1)
                    product(when, name, i, lambda c: W_t[:, i * P:(i + 1) * P], lambda c: dt_in, 1)

            def spread(when, k, i):
                pe.wait_ge(pieces_made, k + 1)
                for j, row in enumerate((2 * i, 2 * i + 1, N + 2 * i, N + 2 * i + 1)):
                    bank, done = open_bank(when, "SPREAD", 4 * i + j)
                    pe.matmul(bank[:, :], choose[:, row:row + 1].to_broadcast([3 * 2 * N, P]), pieces[:, :],
                              start=True, stop=True).then_inc(done, 1)

            def turn_back(when, i, count):
                pe.wait_ge(gated, count)
                bank, done = open_bank(when, "TURN", i)
                for t in range(TT):
                    last = pe.transpose(bank[:, t * P:(t + 1) * P], turnbuf[:, t * P:(t + 1) * P], eye[:, :])
                last.then_inc(done, 1)

            def project(when, i):
                wait_drained(pe, when, "TURN", CT - 1)
                bank, done = open_bank(when, "OUT", i)
                for t in range(2):
                    for c in range(CT):
                        last = pe.matmul(bank[:, t * D:(t + 1) * D], YGT[:, c, (2 * i + t) * P:(2 * i + t + 1) * P],
                                         W_out[:, c, :], start=(c == 0), stop=(c == CT - 1))
                last.then_inc(done, 1)

            def add_step(b, s):
                tile, pair = divmod(s, PAIRS)
                pe.wait_ge(weighted, PAIRS + STEPS * b + s + 1)
                if pair == 0:
                    pe.wait_ge(gated, CT * b + tile + 1)
                if pair == PAIRS - 1:
                    pe.wait_ge(skip_made, 1 + CT * b + tile + 1)
                    for t in range(TT):
                        pe.matmul(yT[:, t * P:(t + 1) * P], turnbuf[:, t * P:(t + 1) * P], eye[:, :],
                                  is_transpose=True, start=False, stop=False, skip_group_check=True)
                for j in range(2):
                    for t in range(TT):
                        last = pe.matmul(yT[:, t * P:(t + 1) * P], h[:, s % RING, j, t * P:(t + 1) * P], eye[:, :],
                                         is_transpose=True, start=(pair == 0 and j == 0 and t == 0),
                                         stop=(pair == PAIRS - 1 and j == 1), skip_group_check=True)
                last.then_inc(summed, 1)

            pe.wait_ge(weights_in, 16 * 13)
            pe.wait_ge(ints_made, 3)
            pe.wait_ge(consts_made, 2)
            pe.wait_ge(a_made, 1)
            for name, i in first_order:
                if name != "SPREAD":
                    stage((None, 0), name, i, 0)
                elif i % 4 == 0:
                    spread((None, 0), 0, i // 4)
            with pe.Fori(0, NB) as b:
                for s in range(STEPS):
                    for name, i in SLOT_FILLS.get(s, []):
                        if name == "SPREAD":
                            spread((b, 0), b + 1 if i < AHEAD else b, i)
                        elif name == "TURN":
                            turn_back((b, 0), i, CT * b + (1 if i == CT - 1 else i + 2))
                        elif name == "OUT":
                            project((b, 0), i)
                        else:
                            stage((b, 0), name, i, b if (name, i) == ("DT", CT - 1) else b + 1)
                    add_step(b, s)
            turn_back(("end", 0), CT - 1, CT * NB + 1)
            project(("end", 0), 0)
            project(("end", 0), 1)

        @block.scalar
        def _(act):
            def copy_out(when, name, i, target):
                bank, done = wait_filled(act, when, name, i)
                nc.scalar.activation(target, bank[:, :], ACT.Copy).then_inc(done, 1)

            def stage(when, name, i, k, first=False):
                if name == "LN":
                    copy_out(when, name, i, XNT[:, i, :])
                elif name == "LN2":
                    bank, done = wait_filled(act, when, name, i)
                    nc.scalar.activation(XHT[:, i, :], bank[:, :], ACT.Identity, bias=shift[:, i:i + 1],
                                         scale=gain[:, i:i + 1]).then_inc(done, 1)
                elif name == "GATE":
                    copy_out(when, name, i, HG[:, i, :])
                elif name == "FFNSILU":
                    wait_all_drained(act, when, "GATE", range(HT))
                    nc.scalar.activation(HG[:, :, :], HG[:, :, :], ACT.Silu).then_inc(silu_gate_made, 1)
                    act.preload_act_table_set(TABLES)
                elif name == "XI":
                    if not first:
                        act.wait_ge(delta_made, CT * k)
                    bank, _ = wait_filled(act, when, name, i)
                    nc.scalar.activation(CPRE[:, i, :], bank[:, :], ACT.Identity, bias=conv_bias[:, i:i + 1],
                                         scale=taps[:, i, K - 1:K]).then_inc(conv_scaled, 1)
                elif name == "Z":
                    if i < 2 and not first:
                        act.wait_ge(gated, CT * (k - 1) + i + 2)
                    copy_out(when, name, i, Z[:, i, :] if i < 2 else Zlate[:, i - 2, :])
                elif name == "SILU":
                    wait_all_drained(act, when, "XI", range(CT))
                    if not first:
                        act.wait_ge(skip_made, CT * k)
                    nc.scalar.activation(XC[:, 0:CT - 1, :], CPRE[:, 0:CT - 1, :], ACT.Silu)
                    nc.scalar.activation(late_u, late_u, ACT.Silu).then_inc(u_made, 1)
                    wait_all_drained(act, when, "Z", range(CT))
                    nc.scalar.activation(Z[:, 0:2, :], Z[:, 0:2, :], ACT.Silu)
                    nc.scalar.activation(Zlate, Zlate, ACT.Silu).then_inc(z_silu_made, 1)
                    act.preload_act_table_set(TABLES)
                elif name == "XP":
                    bank, _ = wait_filled(act, when, name, 0)
                    nc.scalar.activation(pieces[:, :], bank[0:3 * 2 * N, :], ACT.Copy)
                    nc.scalar.activation(dt_in, bank[3 * 2 * N:3 * 2 * N + R, :], ACT.Copy).then_inc(high_made, 1)
                elif name == "MID":
                    wait_drained(act, when, "XP", 0)
                    nc.scalar.activation(pieces[32:64, :], rest[32:64, :], ACT.Copy)
                    nc.scalar.activation(mid_low, rest[64:96, :], ACT.Copy).then_inc(mid_made, 1)
                elif name == "LOW":
                    act.wait_ge(rest_made, k + 1)
                    nc.scalar.activation(pieces[64:96, :], rest[64:96, :], ACT.Copy).then_inc(pieces_made, 1)
                elif name == "DT":
                    if not (first and i == 0):
                        act.wait_ge(delta_made, CT * k + i)
                    act.wait_ge(u_made, k + 1)
                    if not first:
                        act.wait_ge(decay_made, 1 + STEPS * (k - 1) + PAIRS * (i + 1))
                    bank, done = wait_filled(act, when, name, i)
                    nc.scalar.activation(t_e, bank[:, :], ACT.Abs, bias=step_bias[:, i:i + 1]).then_inc(softplus_step, 1)
                    nc.scalar.activation(DELTA[:, i, :], bank[:, :], ACT.Relu, bias=step_bias[:, i:i + 1]).then_inc(done, 1)
                    n = 3 * (CT * k + i)
                    act.wait_ge(softplus_step, n + 1)
                    nc.scalar.activation(t_e, t_e, ACT.Exp, scale=-1.0).then_inc(softplus_step, 1)
                    act.wait_ge(softplus_step, n + 2)
                    nc.scalar.activation(t_u, t_e, ACT.Square, bias=c_bias[:, 0:1], scale=THIRD_ROOT)
                    nc.scalar.activation(t_l, t_e, ACT.Relu, bias=c_bias[:, 1:2]).then_inc(softplus_step, 1)
                    act.wait_ge(softplus_step, n + 3)
                    nc.scalar.activation(t_l, t_l, ACT.Ln, bias=c_bias[:, 2:3]).then_inc(softplus_parts, 1)

            def spread(when, k, i):
                act.wait_ge(drive_made, STEPS * k + i + 1)
                bank, done = wait_filled(act, when, "SPREAD", 4 * i)
                nc.scalar.activation(Bs[:, 2 * i, :], bank[:, :], ACT.Copy).then_inc(done, 1)
                bank, done = wait_filled(act, when, "SPREAD", 4 * i + 1)
                nc.scalar.activation(Bs[:, 2 * i + 1, :], bank[:, :], ACT.Copy).then_inc(done, 1)
                act.wait_ge(weighted, STEPS * k + i + 1)
                bank, done = wait_filled(act, when, "SPREAD", 4 * i + 2)
                nc.scalar.activation(Cs[:, 2 * i, :], bank[:, :], ACT.Copy).then_inc(done, 1)
                bank, done = wait_filled(act, when, "SPREAD", 4 * i + 3)
                nc.scalar.activation(Cs[:, 2 * i + 1, :], bank[:, :], ACT.Copy).then_inc(done, 1)

            def decays(b, s):
                tile, pair = divmod(s, PAIRS)
                if pair == 0:
                    act.wait_ge(delta_made, CT * b + tile + 1)
                act.wait_ge(scanned, STEPS * b + s + 1)
                for j in range(2):
                    n = 2 * pair + j
                    last = nc.scalar.activation(decay[:, s % RING, j, 1:L], DELTA[:, tile, 1:L], ACT.Exp,
                                                scale=negA[:, tile, n:n + 1])
                last.then_inc(decay_made, 1)

            act.wait_ge(weights_in, 16 * 13)
            act.preload_act_table_set(TABLES)
            nc.scalar.activation(choose[:, :], pick_in[:, :], ACT.Copy).then_inc(a_made, 1)
            nc.scalar.activation(negA[:, :, :], negA[:, :, :], ACT.Exp).then_inc(a_made, 1)
            act.wait_ge(a_made, 2)
            nc.scalar.activation(negA[:, :, :], negA[:, :, :], ACT.Copy, scale=-1.0).then_inc(a_made, 1)
            act.wait_ge(a_made, 3)
            act.wait_ge(consts_made, 2)
            act.wait_ge(ints_made, 3)
            for name, i in first_order:
                if name == "UP" and i == 0:
                    stage((None, 0), "FFNSILU", 0, 0, True)
                if name == "XP":
                    stage((None, 0), "SILU", 0, 0, True)
                if name not in ("UP", "DOWN", "SPREAD"):
                    stage((None, 0), name, i, 0, True)
                if name == "XP":
                    stage((None, 0), "MID", 0, 0, True)
                    stage((None, 0), "LOW", 0, 0, True)
            with act.Fori(0, NB) as b:
                for s in range(STEPS):
                    for name, i in ACT_SLOTS.get(s, []):
                        if name == "SPREAD":
                            spread((b, 1) if i < AHEAD else (b, 0), b, i)
                    decays(b, s)
                    for name, i in ACT_SLOTS.get(s, []):
                        if name == "XC3":
                            act.wait_ge(u_made, b + 1)
                            act.wait_ge(skip_made, 1 + CT * b)
                            nc.scalar.activation(XC[:, CT - 1, :], late_u, ACT.Copy).then_inc(u_moved, 1)
                        elif name == "ZCOPY":
                            act.wait_ge(z_silu_made, b + 1)
                            act.wait_ge(gated, CT * b + 1)
                            nc.scalar.activation(Z[:, 2:4, :], Zlate, ACT.Copy).then_inc(z_made, 1)
                        elif name == "TURN":
                            copy_out((b, 0), "TURN", i, YGT[:, i, :])
                        elif name != "SPREAD":
                            stage((b, 0), name, i, b if (name, i) == ("DT", CT - 1) else b + 1)
            for i in range(AHEAD):
                spread((NB, 1), NB, i)
            copy_out(("end", 0), "TURN", CT - 1, YGT[:, CT - 1, :])

        @block.vector
        def _(dve):
            def stage(when, name, i, k, first=False):
                if name == "STATS":
                    dve.wait_ge(x_in, 16 * k + 16)
                    for t in range(TT):
                        last = nc.vector.bn_stats(stats[:, t, :], X[:, t, :])
                    last.then_inc(stats_seen, 1)
                    dve.wait_ge(stats_seen, 2 * k + 1)
                    nc.vector.memset(spare[:, 0:1], 0.0)
                    for t in range(TT):
                        last = nc.vector.bn_aggr(moments[:, t, :], stats[:, t, :])
                    last.then_inc(moments_made, 1)
                elif name == "XN":
                    if not first:
                        dve.wait_ge(z_made, 1 + k)
                    dve.wait_ge(rstd_made, 2 * k + 1)
                    for t in range(TT):
                        last = nc.vector.tensor_scalar(XN[:, t, :], X[:, t, :], moments[:, t, 0:1], rstd[:, 0, t:t + 1],
                                                       ALU.subtract, ALU.mult)
                    last.then_inc(xn_made, 1)
                    dve.wait_ge(xn_made, k + 1)
                    for t in range(TT):
                        last = nc.vector.bn_stats(stats[:, t, :], XN[:, t, :])
                    last.then_inc(stats_seen, 1)
                    dve.wait_ge(stats_seen, 2 * k + 2)
                    nc.vector.memset(spare[:, 0:1], 0.0)
                    for t in range(TT):
                        last = nc.vector.bn_aggr(moments[:, t, :], stats[:, t, :])
                    last.then_inc(moments_made, 1)
                elif name == "XN2":
                    dve.wait_ge(rstd_made, 2 * k + 2)
                    dve.wait_ge(sum_made, k + 1)
                    bank, n = at_fill(when, "LN", KD - 1)
                    dve.wait_ge(filled[bank], n)
                    for t in range(TT):
                        last = nc.vector.tensor_scalar(XN[:, t, :], XN[:, t, :], moments[:, t, 0:1], rstd[:, 1, t:t + 1],
                                                       ALU.subtract, ALU.mult)
                    last.then_inc(xh_made, 1)
                elif name == "XI":
                    bank, done = wait_filled(dve, when, name, i)
                    dve.wait_ge(conv_scaled, CT * k + i + 1)
                    for j in range(1, K):
                        if j > 1:
                            dve.wait_ge(conv_step, 2 * (CT * k + i) + j - 1)
                        nc.vector.scalar_tensor_tensor(
                            out=CPRE[:, i, j:L], in0=bank[:, 0:L - j], scalar=taps[:, i, K - 1 - j:K - j],
                            in1=CPRE[:, i, j:L], op0=ALU.mult, op1=ALU.add,
                        ).then_inc(done if j == K - 1 else conv_step, 1)
                elif name == "UP":
                    if i == 0:
                        dve.wait_ge(silu_gate_made, k + 1)
                    bank, done = wait_filled(dve, when, name, i)
                    nc.vector.tensor_tensor(HG[:, i, :], bank[:, :], HG[:, i, :], ALU.mult).then_inc(done, 1)
                elif name == "DOWN":
                    if i == 0:
                        dve.wait_ge(sum_made, k + 1)
                        if not first:
                            dve.wait_ge(stored, 16 * k)
                    bank, done = wait_filled(dve, when, name, i)
                    nc.vector.tensor_tensor(
                        RES[:, 2 * i:2 * i + 2, :].rearrange("p t d -> p (t d)"), bank[:, :],
                        X[:, 2 * i:2 * i + 2, :].rearrange("p t d -> p (t d)"), ALU.add).then_inc(done, 1)
                elif name == "XP":
                    dve.wait_ge(high_made, k + 1)
                    bank, done = wait_filled(dve, when, name, 0)
                    nc.vector.tensor_tensor(rest[0:96, :], bank[0:96, :], pieces[:, :], ALU.subtract).then_inc(done, 1)
                elif name == "LOW":
                    dve.wait_ge(mid_made, k + 1)
                    nc.vector.tensor_tensor(rest[64:96, :], rest[64:96, :], mid_low, ALU.subtract).then_inc(rest_made, 1)
                elif name == "DT":
                    n = CT * k + i
                    dve.wait_ge(softplus_parts, n + 1)
                    nc.vector.scalar_tensor_tensor(out=t_u, in0=t_u, scalar=13.0 / 16.0, in1=t_e,
                                                   op0=ALU.add, op1=ALU.mult).then_inc(delta_step, 1)
                    dve.wait_ge(delta_step, 2 * n + 1)
                    nc.vector.tensor_tensor(t_u, t_u, t_l, ALU.min).then_inc(delta_step, 1)
                    dve.wait_ge(delta_step, 2 * n + 2)
                    nc.vector.tensor_tensor(DELTA[:, i, :], DELTA[:, i, :], t_u, ALU.add).then_inc(delta_made, 1)

            def gate_y(i, summed_count, z_count):
                dve.wait_ge(summed, summed_count)
                dve.wait_ge(z_made, 1 + z_count)
                nc.vector.tensor_tensor(turnbuf[:, :], yT[:, :], Z[:, i, :], ALU.mult).then_inc(gated, 1)

            def finish(when, b, i):
                if i == 0:
                    dve.wait_ge(spilled, 16 * min(b + 1, NB) if isinstance(when[0], str) else 16 * b + 16)
                    dve.wait_ge(reloaded, 16 * b + 16)
                bank, done = wait_filled(dve, when, "OUT", i)
                res = RES[:, 2 * i:2 * i + 2, :].rearrange("p t d -> p (t d)")
                nc.vector.tensor_tensor(res, bank[:, :], res, ALU.add).then_inc(done, 1)

            def start_tile(b, tile):
                dve.wait_ge(delta_made, CT * b + tile + 1)
                dve.wait_ge(u_moved, b + 1)
                dve.wait_ge(drive_made, STEPS * b + PAIRS * (tile + 1))
                nc.vector.tensor_tensor(du[:, 0, :], DELTA[:, tile, :], XC[:, tile, :], ALU.mult).then_inc(du_made, 1)

            def drives(b, s):
                tile, pair = divmod(s, PAIRS)
                if pair == 0:
                    start_tile(b, tile)
                    dve.wait_ge(du_made, CT * b + tile + 1)
                if tile == 0:
                    for j in (0, 1):
                        wait_drained(dve, (b, 1) if pair < AHEAD else (b, 0), "SPREAD", 4 * pair + j)
                dve.wait_ge(scanned, RING + STEPS * b + s - 1)
                nc.vector.tensor_tensor(drive[:, s % 2, :, :], du[:, :, :].to_broadcast([P, 2, L]),
                                        Bs[:, 2 * pair:2 * pair + 2, :], ALU.mult).then_inc(drive_made, 1)

            def scan(b, s):
                dve.wait_ge(drive_made, PAIRS + STEPS * b + s + 1)
                dve.wait_ge(decay_made, 1 + STEPS * b + s + 1)
                dve.wait_ge(summed, STEPS * b + s + 1)
                nc.vector.tensor_tensor_scan(
                    h[:, s % RING, :, :].rearrange("p a b -> p (a b)"),
                    decay[:, s % RING, :, :].rearrange("p a b -> p (a b)"),
                    drive[:, s % 2, :, :].rearrange("p a b -> p (a b)"), 0.0, ALU.mult, ALU.add).then_inc(scanned, 1)

            nc.vector.memset(decay[:, :, :, 0:1], 0.0).then_inc(scanned, RING)
            nc.vector.memset(c_bias[:, 0:1], -0.75 * THIRD_ROOT).then_inc(skip_made, 1)
            nc.vector.memset(c_bias[:, 1:2], -SMALL).then_inc(z_made, 1)
            nc.vector.memset(c_bias[:, 2:3], 1.0 + SMALL).then_inc(consts_made, 1)
            nc.vector.memset(yT[:, :], 0.0).then_inc(summed, RING)
            nc.vector.memset(Z[:, CT - 1, :], 0.0).then_inc(drive_made, PAIRS)
            nc.vector.memset(spare[:, 1:2], 0.0).then_inc(decay_made, 1)
            nc.vector.memset(spare[:, 2:3], 0.0).then_inc(reloaded, 16)
            nc.vector.memset(spare[:, 3:4], 0.0).then_inc(stored, 16)
            dve.wait_ge(ints_in, 48)
            for source, weight in ((HG[:, 0:3, :], W_g), (HG[:, 3:6, :], W_u), (CPRE[:, 0:3, :], W_d)):
                nc.vector.tensor_scalar(weight[:, :, :].rearrange("p k n -> p (k n)"),
                                        source.bitcast(I32).rearrange("p a b -> p (a b)"),
                                        QUANT, None, ALU.mult).then_inc(ints_made, 1)
            stage((None, 0), "STATS", 0, 0, True)
            stage((None, 0), "XN", 0, 0, True)
            stage((None, 0), "XN2", 0, 0, True)
            for name, i in first_order:
                if name in ("XI", "UP", "DOWN", "XP", "DT"):
                    stage((None, 0), name, i, 0, True)
                if name == "XP":
                    stage((None, 0), "LOW", 0, 0, True)
            with dve.Fori(0, NB) as b:
                drives(b, 0)
                for s in range(STEPS):
                    tile, pair = divmod(s, PAIRS)
                    if s + 1 < STEPS:
                        drives(b, s + 1)
                    scan(b, s)
                    for name, i in DVE_SLOTS.get(s, []):
                        if name == "YGATE":
                            before = i == CT - 1
                            gate_y(i, RING + STEPS * b + (0 if before else PAIRS * (i + 1)), b if before else b + 1)
                        elif name == "OUT":
                            finish((b, 0), b, i)
                        else:
                            stage((b, 0), name, i, b if (name, i) == ("DT", CT - 1) else b + 1)
                    if pair == 4:
                        bank, n = at_fill((b, 0), "TURN", (tile - 1) % CT)
                        dve.wait_ge(filled[bank], n)
                        nc.vector.tensor_scalar(turnbuf[:, :], XC[:, tile, :], skip[:, tile:tile + 1], None,
                                                ALU.mult).then_inc(skip_made, 1)
            gate_y(CT - 1, RING + STEPS * NB, NB)
            finish(("end", 0), NB, 0)
            finish(("end", 0), NB, 1)

        @block.gpsimd
        def _(pool):
            def stage(name, i, k):
                if name == "RSTD":
                    pool.wait_ge(moments_made, 2 * k + i + 1)
                    nc.gpsimd.tensor_tensor(rstd[:, i, :], moments[:, :, 1], c_eps[:, TT:2 * TT], ALU.add).then_inc(pow_step, 1)
                    pool.wait_ge(pow_step, 2 * k + i + 1)
                    nc.gpsimd.tensor_tensor(rstd[:, i, :], rstd[:, i, :], c_eps[:, 0:TT], ALU.pow).then_inc(rstd_made, 1)
                else:
                    pool.wait_ge(xn_made, k + 1)
                    nc.gpsimd.tensor_tensor(X[:, :, :], X[:, :, :], XN[:, :, :], ALU.add).then_inc(sum_made, 1)

            def weigh(b, s):
                pair = s % PAIRS
                pool.wait_ge(scanned, RING + STEPS * b + s + 1)
                if s < PAIRS:
                    for j in (2, 3):
                        wait_drained(pool, (b, 1) if pair < AHEAD else (b, 0), "SPREAD", 4 * pair + j)
                hs = h[:, s % RING, :, :]
                nc.gpsimd.tensor_tensor(hs, hs, Cs[:, 2 * pair:2 * pair + 2, :], ALU.mult).then_inc(weighted, 1)

            nc.gpsimd.memset(c_eps[:, TT:2 * TT], EPS)
            nc.gpsimd.memset(c_eps[:, 0:TT], -0.5).then_inc(weighted, PAIRS)
            nc.gpsimd.memset(YGT[:, 0:CT - 1, :], 0.0).then_inc(consts_made, 1)
            pool.wait_ge(weighted, PAIRS)
            stage("RSTD", 0, 0)
            stage("RSTD", 1, 0)
            stage("SUM", 0, 0)
            with pool.Fori(0, NB) as b:
                for s in range(STEPS):
                    weigh(b, s)
                    for name, i in POOL_SLOTS.get(s, []):
                        stage(name, i, b + 1)


def _laid_out(i):
    import numpy as np

    def columns(v):
        return np.ascontiguousarray(np.asarray(v).reshape(-1, P).T)

    def tiles(m):
        return np.ascontiguousarray(np.asarray(m).reshape(-1, P, m.shape[-1]).transpose(1, 0, 2))

    w_xp = np.asarray(i["L0_attn_W_xp"])
    rank = i["L0_attn_W_dt"].shape[0]
    w_bc, w_low = w_xp[:, rank:], w_xp[:, :rank]
    n2 = w_bc.shape[1]
    pick = np.tile(np.eye(n2, dtype=np.float32), (3, 1))
    return {
        "x": np.asarray(i["L0_attn_x"]),
        "ln_g": columns(i["L0_attn_ln_g"]),
        "ln_b": columns(i["L0_attn_ln_b"]),
        "w_in": np.asarray(i["L0_attn_W_in"]),
        "conv_w": tiles(np.asarray(i["L0_attn_conv_w"])[:, 0, :]),
        "conv_b": columns(i["L0_attn_conv_b"]),
        "w_xp": np.concatenate([w_bc, w_bc, w_bc, w_low], axis=1),
        "w_dt": np.asarray(i["L0_attn_W_dt"]),
        "dt_bias": columns(i["L0_attn_dt_bias"]),
        "a_log": tiles(np.asarray(i["L0_attn_A_log"])),
        "d_skip": columns(i["L0_attn_D_skip"]),
        "w_out": np.asarray(i["L0_attn_W_out"]),
        "w_gate": np.ascontiguousarray(np.asarray(i["L0_ffn_w_gate"]).T),
        "w_up": np.ascontiguousarray(np.asarray(i["L0_ffn_w_up"]).T),
        "w_down": np.ascontiguousarray(np.asarray(i["L0_ffn_w_down"]).T),
        "ident": np.eye(P, dtype=np.float32),
        "pick": pick,
    }


def kernel(**inputs):
    import numpy as _np
    import concourse.bacc as _bacc
    from concourse.bass_utils import run_bass_kernel_spmd as _run

    nc = _bacc.Bacc("TRN2", target_bir_lowering=False, num_devices=1)
    arrays, args = {}, []
    for name, a in _laid_out(inputs).items():
        arrays[f"in_{name}"] = a
        args.append(nc.dram_tensor(f"in_{name}", a.shape, mybir.dt.from_np(a.dtype), kind="ExternalInput").ap())
    shape = arrays["in_x"].shape
    args.append(nc.dram_tensor("out_dram", shape, F32, kind="ExternalOutput").ap())
    bass_mamba_ffn_block_kernel(nc, *args)
    r = _run(nc, [arrays], core_ids=[0])
    return r.results[0]["out_dram"]
```

```python
from contextlib import ExitStack

import concourse.bass as bass
from concourse import mybir

ALU = mybir.AluOpType
ACT = mybir.ActivationFunctionType
F32 = mybir.dt.float32
BF16 = mybir.dt.bfloat16
I32 = mybir.dt.int32

P = 128
EPS = 1e-5
QUANT = 1.0 / 127.0
SMALL = 0.02
THIRD_ROOT = 3.0 ** -0.5
TABLES = "natural_log_exp_and_others"

SLOT_FILLS = {
    0: [("SPREAD", 4), ("TURN", 3), ("DT", 3)], 1: [("OUT", 0), ("LN", 0), ("LN", 1)], 2: [("SPREAD", 5)],
    3: [("SPREAD", 6)], 4: [("SPREAD", 7)], 5: [("OUT", 1), ("GATE", 0)], 6: [("GATE", 1), ("GATE", 2)],
    8: [("GATE", 3), ("GATE", 4), ("GATE", 5), ("LN2", 0)], 9: [("LN2", 1), ("TURN", 0)], 10: [("XI", 0)],
    11: [("XI", 1)], 12: [("Z", 0)], 13: [("UP", 0), ("UP", 1)], 15: [("UP", 2)],
    16: [("Z", 1), ("TURN", 1), ("Z", 2)], 17: [("UP", 3), ("Z", 3), ("XI", 2)], 18: [("XI", 3)],
    21: [("UP", 4), ("UP", 5), ("XP", 0)], 22: [("DT", 0)], 24: [("DT", 1), ("DOWN", 0)],
    25: [("TURN", 2), ("DT", 2)], 26: [("DOWN", 1)], 28: [("SPREAD", 0), ("SPREAD", 1)],
    30: [("SPREAD", 2), ("SPREAD", 3)],
}
ACT_SLOTS = {
    0: [("SPREAD", 0), ("SPREAD", 1), ("XC3", 0)], 1: [("SPREAD", 2), ("SPREAD", 3)],
    2: [("SPREAD", 4), ("TURN", 3)], 3: [("ZCOPY", 0)], 4: [("DT", 3), ("LN", 0), ("LN", 1)], 5: [("SPREAD", 5)],
    6: [("SPREAD", 6), ("SPREAD", 7)], 7: [("GATE", 0)], 10: [("GATE", 1)], 11: [("GATE", 2)],
    13: [("GATE", 3), ("GATE", 4)], 14: [("GATE", 5), ("LN2", 0), ("LN2", 1)], 15: [("TURN", 0), ("XI", 0)],
    16: [("XI", 1)], 17: [("Z", 0), ("FFNSILU", 0)], 19: [("Z", 1), ("TURN", 1), ("Z", 2)],
    23: [("Z", 3), ("XI", 2), ("XI", 3)], 25: [("SILU", 0), ("XP", 0)], 26: [("DT", 0)],
    28: [("MID", 0), ("DT", 1), ("TURN", 2)], 31: [("LOW", 0), ("DT", 2)],
}
DVE_SLOTS = {
    0: [("YGATE", 3), ("STATS", 0)], 2: [("XN", 0), ("OUT", 0)], 3: [("DT", 3)], 4: [("XN2", 0)], 7: [("OUT", 1)],
    10: [("YGATE", 0)], 13: [("XI", 0)], 14: [("XI", 1)], 15: [("UP", 0), ("UP", 1)], 16: [("UP", 2), ("YGATE", 1)],
    19: [("UP", 3)], 21: [("XI", 2), ("XI", 3), ("UP", 4)], 23: [("UP", 5)], 24: [("XP", 0)], 25: [("DT", 0)],
    26: [("LOW", 0), ("YGATE", 2), ("DOWN", 0)], 27: [("DT", 1)], 28: [("DOWN", 1)], 31: [("DT", 2)],
}
POOL_SLOTS = {
    0: [("RSTD", 0)], 1: [("SUM", 0)], 3: [("RSTD", 1)], 10: [("DT", 3)], 24: [("DT", 0)], 26: [("DT", 1)],
    30: [("DT", 2)],
}


def bass_mamba_ffn_block_kernel(
    nc: bass.Bass, x: bass.AP, ln_g: bass.AP, ln_b: bass.AP, w_in: bass.AP, conv_w: bass.AP,
    conv_b: bass.AP, w_xp: bass.AP, w_dt: bass.AP, dt_bias: bass.AP, a_log: bass.AP, d_skip: bass.AP,
    w_out: bass.AP, w_gate: bass.AP, w_up: bass.AP, w_down: bass.AP, ident: bass.AP, pick: bass.AP,
    out: bass.AP,
):
    NB, L, D = x.shape
    DI = w_out.shape[0]
    N = a_log.shape[-1]
    R = w_dt.shape[0]
    K = conv_w.shape[-1]
    HID = w_gate.shape[-1]
    TT, KD, CT, HT = L // P, D // P, DI // P, HID // P
    PAIRS = N // 2
    STEPS = CT * PAIRS
    RING = 4
    AHEAD = 4
    SKIP_PAIR = 4
    POOL_PAIRS = (3, 7)
    OWN_PAIRS = tuple(p for p in range(PAIRS) if p not in POOL_PAIRS)
    LEAD = 3
    POOL_TILE, OWN_TILE = len(POOL_PAIRS), len(OWN_PAIRS)
    assert L == 512 and 3 * 2 * N + R <= P and STEPS % RING == 0

    order = []
    for s in range(STEPS):
        for name, i in SLOT_FILLS.get(s, []):
            order += [("SPREAD", 4 * i + j) for j in range(4)] if name == "SPREAD" else [(name, i)]
    stage_names = ("LN", "LN2", "GATE", "XI", "Z", "UP", "XP", "DOWN", "DT", "SPREAD")
    def opening(name, i):
        return name in stage_names and (name, i) != ("DT", CT - 1) and not (name == "SPREAD" and i >= 4 * AHEAD)
    first_order = [f for f in order if opening(*f)]
    closing_order = [("TURN", CT - 1), ("OUT", 0), ("OUT", 1)]
    def places(fills, last_bank):
        banks = [(last_bank - (len(fills) - 1 - n)) % 2 for n in range(len(fills))]
        at, used = {}, [0, 0]
        for f, bank in zip(fills, banks):
            used[bank] += 1
            at[f] = (bank, used[bank])
        return at, used
    for earlier, later in (
        (("TURN", CT - 1), ("OUT", 0)), (("OUT", 1), ("TURN", 0)), (("DT", CT - 1), ("LN", 0)),
        (("LN", KD - 1), ("GATE", 0)), (("LN2", KD - 1), ("XI", 0)), (("XI", 0), ("Z", 0)),
        (("UP", HT - 1), ("XP", 0)), (("XI", CT - 1), ("XP", 0)),
    ):
        assert order.index(earlier) < order.index(later)
    in_pass, per_pass = places(order, 0)
    in_first, per_first = places(first_order, 0)
    in_closing, _ = places(closing_order, 0)

    ctx = ExitStack()
    with ctx:
        def sb(name, shape, dt=F32):
            return ctx.enter_context(nc.sbuf_tensor(name, shape, dt))

        def ps(name, shape):
            return ctx.enter_context(nc.psum_tensor(name, shape, F32))

        def sem(name):
            return ctx.enter_context(nc.semaphore(name))

        W_in = sb("W_in", [P, KD, 2 * DI])
        W_out = sb("W_out", [P, CT, D])
        W_g = sb("W_g", [P, KD, HID])
        W_u = sb("W_u", [P, KD, HID])
        W_d = sb("W_d", [P, HT, D])
        W_x = sb("W_x", [P, CT, 3 * 2 * N + R])
        W_t = sb("W_t", [R, DI])
        eye = sb("eye", [P, P])
        choose = sb("choose", [3 * 2 * N, 2 * N], BF16)
        gain = sb("gain", [P, KD])
        shift = sb("shift", [P, KD])
        taps = sb("taps", [P, CT, K])
        conv_bias = sb("conv_bias", [P, CT])
        step_bias = sb("step_bias", [P, CT])
        skip = sb("skip", [P, CT])
        SKIP = sb("SKIP", [P, CT, P])
        negA = sb("negA", [P, CT, N])
        pick_in = sb("pick_in", [3 * 2 * N, 2 * N])
        c_eps = sb("c_eps", [P, 2 * TT])
        spare = sb("spare", [P, 4])
        c_bias = sb("c_bias", [P, 3])

        X = sb("X", [P, TT, D])
        XN = sb("XN", [P, TT, D])
        XNT = sb("XNT", [P, KD, L])
        XHT = sb("XHT", [P, KD, L])
        stats = sb("stats", [P, TT, 6])
        moments = sb("moments", [P, TT, 2])
        rstd = sb("rstd", [P, 2, TT])
        HG = sb("HG", [P, HT, L])
        CPRE = sb("CPRE", [P, CT, L])
        XC = sb("XC", [P, CT, L])
        DELTA = sb("DELTA", [P, CT, L])
        Z = sb("Z", [P, CT, TT * P])
        pieces = sb("pieces", [3 * 2 * N, L], BF16)
        Bs = sb("Bs", [P, N, L])
        Cs = sb("Cs", [P, N, L])
        YGT = sb("YGT", [P, CT, L])

        decay = sb("decay", [P, RING, 2, L])
        h = sb("h", [P, RING, 2, L])
        du_copy = sb("du_copy", [P, 1, L])
        turnbuf = sb("turnbuf", [P, L])

        RES = XHT[:, :, :].rearrange("p a b -> p (a b)").rearrange("p (t d) -> p t d", t=TT)
        Zlate = XN[:, :, :].rearrange("p a b -> p (a b)").rearrange("p (c f) -> p c f", c=2)
        rest = XNT[:, 0, :]
        dt_in = XNT[0:R, 1, :]
        mid_low = XNT[64:64 + 2 * N, 1, 0:L // 2].bitcast(BF16)
        t_e, t_l, t_u = CPRE[:, 0, :], CPRE[:, 1, :], CPRE[:, 2, :]
        late_u = CPRE[:, CT - 1, :]

        general = [ps("general0", [P, L]), ps("general1", [P, L])]
        yT = ps("yT", [P, TT * P])
        du = ps("du", [P, 1, L])
        drive = ps("drive", [P, 2, 2, L])

        filled = [sem("filled0"), sem("filled1")]
        drained = [sem("drained0"), sem("drained1")]
        weights_in = sem("weights_in")
        ints_in = sem("ints_in")
        ints_made = sem("ints_made")
        a_made = sem("a_made")
        x_in = sem("x_in")
        consts_made = sem("consts_made")
        stats_seen = sem("stats_seen")
        moments_made = sem("moments_made")
        pow_step = sem("pow_step")
        rstd_made = sem("rstd_made")
        xn_made = sem("xn_made")
        xh_made = sem("xh_made")
        sum_made = sem("sum_made")
        silu_gate_made = sem("silu_gate_made")
        conv_step = sem("conv_step")
        conv_scaled = sem("conv_scaled")
        u_made = sem("u_made")
        u_moved = sem("u_moved")
        z_silu_made = sem("z_silu_made")
        z_made = sem("z_made")
        high_made = sem("high_made")
        mid_made = sem("mid_made")
        rest_made = sem("rest_made")
        pieces_made = sem("pieces_made")
        softplus_step = sem("softplus_step")
        softplus_parts = sem("softplus_parts")
        delta_step = sem("delta_step")
        delta_made = sem("delta_made")
        du_made = sem("du_made")
        decay_made = sem("decay_made")
        drive_made = sem("drive_made")
        du_copied = sem("du_copied")
        pool_drive_made = sem("pool_drive_made")
        scanned = sem("scanned")
        weighted = sem("weighted")
        summed = sem("summed")
        gated = sem("gated")
        spilled = sem("spilled")
        reloaded = sem("reloaded")
        stored = sem("stored")

        x_v = x.rearrange("b (t p) d -> b p t d", p=P)
        out_v = out.rearrange("b (t p) d -> b p t d", p=P)

        def at_fill(when, name, i):
            b, late = when
            if b is None:
                return in_first[name, i]
            if isinstance(b, str):
                bank, n = in_closing[name, i]
                return bank, per_first[bank] + NB * per_pass[bank] + n
            bank, n = in_pass[name, i]
            base = per_first[bank] + n - (per_pass[bank] if late else 0)
            assert base > 0 and (not late or name != "SPREAD" or in_first[name, i] == (bank, base))
            return bank, per_pass[bank] * b + base

        def wait_filled(eng, when, name, i):
            bank, n = at_fill(when, name, i)
            eng.wait_ge(filled[bank], n)
            return general[bank], drained[bank]

        def wait_drained(eng, when, name, i):
            bank, n = at_fill(when, name, i)
            eng.wait_ge(drained[bank], n)

        def wait_all_drained(eng, when, *fills):
            latest = {}
            for name, which in fills:
                for i in range(which):
                    bank, n = (in_closing if isinstance(when[0], str) else in_pass)[name, i]
                    if bank not in latest or n > latest[bank][0]:
                        latest[bank] = (n, name, i)
            for n, name, i in latest.values():
                wait_drained(eng, when, name, i)

        block = ctx.enter_context(nc.Block())

        @block.sync
        def _(sp):
            sp.dma_start(HG[:, 0:3, :].bitcast(I32).rearrange("p a b -> p (a b)").rearrange("p (k n) -> p k n", k=KD),
                         w_gate.rearrange("(k p) n -> p k n", p=P)).then_inc(ints_in, 16)
            sp.dma_start(HG[:, 3:6, :].bitcast(I32).rearrange("p a b -> p (a b)").rearrange("p (k n) -> p k n", k=KD),
                         w_up.rearrange("(k p) n -> p k n", p=P)).then_inc(ints_in, 16)
            sp.dma_start(CPRE[:, 0:3, :].bitcast(I32).rearrange("p a b -> p (a b)").rearrange("p (k n) -> p k n", k=HT),
                         w_down.rearrange("(k p) n -> p k n", p=P)).then_inc(ints_in, 16)
            sp.dma_start(X[:, :, :], x_v[0]).then_inc(x_in, 16)
            sp.dma_start(eye[:, :], ident).then_inc(weights_in, 16)
            sp.dma_start(W_in[:, :, :], w_in.rearrange("(k p) n -> p k n", p=P)).then_inc(weights_in, 16)
            sp.dma_start(W_out[:, :, :], w_out.rearrange("(k p) n -> p k n", p=P)).then_inc(weights_in, 16)
            sp.dma_start(W_x[:, :, :], w_xp.rearrange("(k p) n -> p k n", p=P)).then_inc(weights_in, 16)
            sp.dma_start(W_t[:, :], w_dt).then_inc(weights_in, 16)
            sp.dma_start(pick_in[:, :], pick).then_inc(weights_in, 16)
            for tile, vector in ((gain, ln_g), (shift, ln_b), (conv_bias, conv_b), (step_bias, dt_bias), (skip, d_skip)):
                sp.dma_start(tile[:, :], vector).then_inc(weights_in, 16)
            sp.dma_start(taps[:, :, :], conv_w).then_inc(weights_in, 16)
            sp.dma_start(negA[:, :, :], a_log).then_inc(weights_in, 16)

            def spill(when, row):
                wait_drained(sp, when, "DOWN", 1)
                sp.dma_start(out_v[row], X[:, :, :]).then_inc(spilled, 16)

            def load_x(row, spills):
                sp.wait_ge(spilled, 16 * spills)
                sp.dma_start(X[:, :, :], x_v[row]).then_inc(x_in, 16)

            def finish(when, b, row):
                sp.wait_ge(spilled, 16 * b)
                wait_all_drained(sp, (b, 1), ("XI", CT), ("Z", CT))
                sp.dma_start(RES[:, :, :], out_v[row]).then_inc(reloaded, 16)
                wait_drained(sp, when, "OUT", 1)
                sp.dma_start(out_v[row], RES[:, :, :]).then_inc(stored, 16)

            spill((None, 0), 0)
            load_x(1, 1)
            spill((0, 0), 1)
            load_x(2, 2)
            with sp.Fori(1, NB - 2) as b:
                finish((b, 0), b, b - 1)
                spill((b, 0), b + 1)
                load_x(b + 2, b + 2)
            finish((NB - 2, 0), NB - 2, NB - 3)
            spill((NB - 2, 0), NB - 1)
            load_x(NB - 1, NB)
            finish((NB - 1, 0), NB - 1, NB - 2)
            finish(("end", 0), NB, NB - 1)
            sp.wait_ge(stored, 16 * (NB + 1))

        @block.tensor
        def _(pe):
            def open_bank(when, name, i):
                bank, n = at_fill(when, name, i)
                if not (when[0] is None and n == 1):
                    pe.wait_ge(drained[bank], n - 1)
                return general[bank], filled[bank]

            def turned(when, name, i, k):
                pe.wait_ge(xn_made if name == "LN" else xh_made, k + 1)
                bank, done = open_bank(when, name, i)
                for t in range(TT):
                    last = pe.transpose(bank[:, t * P:(t + 1) * P], XN[:, t, i * P:(i + 1) * P], eye[:, :])
                last.then_inc(done, 1)

            def product(when, name, i, weight, moving, tiles):
                bank, done = open_bank(when, name, i)
                for c in range(tiles):
                    w = weight(c)
                    last = pe.matmul(bank[0:w.shape[-1], :], w, moving(c), start=(c == 0), stop=(c == tiles - 1))
                last.then_inc(done, 1)

            def stage(when, name, i, k):
                if name in ("LN", "LN2"):
                    turned(when, name, i, k)
                elif name == "GATE":
                    if i == 0:
                        wait_all_drained(pe, when, ("LN", KD))
                    product(when, name, i, lambda c: W_g[:, c, i * P:(i + 1) * P], lambda c: XNT[:, c, :], KD)
                elif name == "UP":
                    product(when, name, i, lambda c: W_u[:, c, i * P:(i + 1) * P], lambda c: XNT[:, c, :], KD)
                elif name == "XI":
                    if i == 0:
                        wait_all_drained(pe, when, ("LN2", KD))
                    product(when, name, i, lambda c: W_in[:, c, i * P:(i + 1) * P], lambda c: XHT[:, c, :], KD)
                elif name == "Z":
                    bank, done = open_bank(when, name, i)
                    for t in range(TT):
                        for c in range(KD):
                            last = pe.matmul(bank[:, t * P:(t + 1) * P], XHT[:, c, t * P:(t + 1) * P],
                                             W_in[:, c, DI + i * P:DI + (i + 1) * P],
                                             start=(c == 0), stop=(c == KD - 1))
                    last.then_inc(done, 1)
                elif name == "XP":
                    pe.wait_ge(u_made, k + 1)
                    product(when, name, 0, lambda c: W_x[:, c, :],
                            lambda c: late_u if c == CT - 1 else XC[:, c, :], CT)
                elif name == "DOWN":
                    wait_all_drained(pe, when, ("UP", HT))
                    bank, done = open_bank(when, name, i)
                    for t in range(2):
                        for c in range(HT):
                            last = pe.matmul(bank[:, t * D:(t + 1) * D], HG[:, c, (2 * i + t) * P:(2 * i + t + 1) * P],
                                             W_d[:, c, :], start=(c == 0), stop=(c == HT - 1))
                    last.then_inc(done, 1)
                elif name == "DT":
                    pe.wait_ge(high_made, k + 1)
                    product(when, name, i, lambda c: W_t[:, i * P:(i + 1) * P], lambda c: dt_in, 1)

            def spread(when, k, i):
                pe.wait_ge(pieces_made, k + 1)
                for j, row in enumerate((2 * i, 2 * i + 1, N + 2 * i, N + 2 * i + 1)):
                    bank, done = open_bank(when, "SPREAD", 4 * i + j)
                    pe.matmul(bank[:, :], choose[:, row:row + 1].to_broadcast([3 * 2 * N, P]), pieces[:, :],
                              start=True, stop=True).then_inc(done, 1)

            def turn_back(when, i, count):
                pe.wait_ge(gated, count)
                bank, done = open_bank(when, "TURN", i)
                for t in range(TT):
                    last = pe.transpose(bank[:, t * P:(t + 1) * P], turnbuf[:, t * P:(t + 1) * P], eye[:, :])
                last.then_inc(done, 1)

            def project(when, i):
                wait_drained(pe, when, "TURN", CT - 1)
                bank, done = open_bank(when, "OUT", i)
                for t in range(2):
                    for c in range(CT):
                        last = pe.matmul(bank[:, t * D:(t + 1) * D], YGT[:, c, (2 * i + t) * P:(2 * i + t + 1) * P],
                                         W_out[:, c, :], start=(c == 0), stop=(c == CT - 1))
                last.then_inc(done, 1)

            def add_step(b, s):
                tile, pair = divmod(s, PAIRS)
                pe.wait_ge(weighted, PAIRS + STEPS * b + s + 1)
                if pair == 0:
                    pe.wait_ge(gated, CT * b + tile + 1)
                if pair == SKIP_PAIR:
                    pe.wait_ge(u_moved, b + 1)
                    for t in range(TT):
                        pe.matmul(yT[:, t * P:(t + 1) * P], XC[:, tile, t * P:(t + 1) * P], SKIP[:, tile, :],
                                  start=False, stop=False, skip_group_check=True)
                for j in range(2):
                    for t in range(TT):
                        last = pe.matmul(yT[:, t * P:(t + 1) * P], h[:, s % RING, j, t * P:(t + 1) * P], eye[:, :],
                                         is_transpose=True, start=(pair == 0 and j == 0 and t == 0),
                                         stop=(pair == PAIRS - 1 and j == 1), skip_group_check=True)
                last.then_inc(summed, 1)

            pe.wait_ge(weights_in, 16 * 13)
            pe.wait_ge(ints_made, 4)
            pe.wait_ge(consts_made, 3)
            pe.wait_ge(a_made, 1)
            for name, i in first_order:
                if name != "SPREAD":
                    stage((None, 0), name, i, 0)
                elif i % 4 == 0:
                    spread((None, 0), 0, i // 4)
            with pe.Fori(0, NB) as b:
                for s in range(STEPS):
                    for name, i in SLOT_FILLS.get(s, []):
                        if name == "SPREAD":
                            spread((b, 0), b + 1 if i < AHEAD else b, i)
                        elif name == "TURN":
                            turn_back((b, 0), i, CT * b + (1 if i == CT - 1 else i + 2))
                        elif name == "OUT":
                            project((b, 0), i)
                        else:
                            stage((b, 0), name, i, b if (name, i) == ("DT", CT - 1) else b + 1)
                    add_step(b, s)
            turn_back(("end", 0), CT - 1, CT * NB + 1)
            project(("end", 0), 0)
            project(("end", 0), 1)

        @block.scalar
        def _(act):
            def copy_out(when, name, i, target):
                bank, done = wait_filled(act, when, name, i)
                nc.scalar.activation(target, bank[:, :], ACT.Copy).then_inc(done, 1)

            def stage(when, name, i, k, first=False, silu_next=False):
                if name == "LN":
                    copy_out(when, name, i, XNT[:, i, :])
                elif name == "LN2":
                    if not first:
                        act.wait_ge(stored, 16 * k)
                    bank, done = wait_filled(act, when, name, i)
                    nc.scalar.activation(XHT[:, i, :], bank[:, :], ACT.Identity, bias=shift[:, i:i + 1],
                                         scale=gain[:, i:i + 1]).then_inc(done, 1)
                elif name == "GATE":
                    copy_out(when, name, i, HG[:, i, :])
                elif name == "FFNSILU":
                    wait_all_drained(act, when, ("GATE", HT))
                    nc.scalar.activation(HG[:, :, :], HG[:, :, :], ACT.Silu).then_inc(silu_gate_made, 1)
                    if not silu_next:
                        act.preload_act_table_set(TABLES)
                elif name == "XI":
                    if not first:
                        act.wait_ge(delta_made, CT * k)
                    bank, _ = wait_filled(act, when, name, i)
                    nc.scalar.activation(CPRE[:, i, :], bank[:, :], ACT.Identity, bias=conv_bias[:, i:i + 1],
                                         scale=taps[:, i, K - 1:K]).then_inc(conv_scaled, 1)
                elif name == "Z":
                    if i < 2 and not first:
                        act.wait_ge(gated, CT * (k - 1) + i + 2)
                    copy_out(when, name, i, Z[:, i, :] if i < 2 else Zlate[:, i - 2, :])
                elif name == "SILU":
                    wait_all_drained(act, when, ("XI", CT))
                    if not first:
                        act.wait_ge(summed, RING + STEPS * (k - 1) + PAIRS * (CT - 2) + SKIP_PAIR + 1)
                    nc.scalar.activation(XC[:, 0:CT - 1, :], CPRE[:, 0:CT - 1, :], ACT.Silu)
                    nc.scalar.activation(late_u, late_u, ACT.Silu).then_inc(u_made, 1)
                    wait_all_drained(act, when, ("Z", CT))
                    nc.scalar.activation(Z[:, 0:2, :], Z[:, 0:2, :], ACT.Silu)
                    nc.scalar.activation(Zlate, Zlate, ACT.Silu).then_inc(z_silu_made, 1)
                    if not silu_next:
                        act.preload_act_table_set(TABLES)
                elif name == "XP":
                    bank, _ = wait_filled(act, when, name, 0)
                    nc.scalar.activation(pieces[:, :], bank[0:3 * 2 * N, :], ACT.Copy)
                    nc.scalar.activation(dt_in, bank[3 * 2 * N:3 * 2 * N + R, :], ACT.Copy).then_inc(high_made, 1)
                elif name == "MID":
                    wait_drained(act, when, "XP", 0)
                    nc.scalar.activation(pieces[32:64, :], rest[32:64, :], ACT.Copy)
                    nc.scalar.activation(mid_low, rest[64:96, :], ACT.Copy).then_inc(mid_made, 1)
                elif name == "LOW":
                    act.wait_ge(rest_made, k + 1)
                    nc.scalar.activation(pieces[64:96, :], rest[64:96, :], ACT.Copy).then_inc(pieces_made, 1)
                elif name == "DT":
                    if not (first and i == 0):
                        act.wait_ge(delta_made, CT * k + i)
                    act.wait_ge(u_made, k + 1)
                    if not first:
                        act.wait_ge(decay_made, 1 + STEPS * (k - 1) + PAIRS * (i + 1))
                    bank, done = wait_filled(act, when, name, i)
                    nc.scalar.activation(t_e, bank[:, :], ACT.Abs, bias=step_bias[:, i:i + 1]).then_inc(softplus_step, 1)
                    nc.scalar.activation(DELTA[:, i, :], bank[:, :], ACT.Relu, bias=step_bias[:, i:i + 1]).then_inc(done, 1)
                    n = 3 * (CT * k + i)
                    act.wait_ge(softplus_step, n + 1)
                    nc.scalar.activation(t_e, t_e, ACT.Exp, scale=-1.0).then_inc(softplus_step, 1)
                    act.wait_ge(softplus_step, n + 2)
                    nc.scalar.activation(t_u, t_e, ACT.Square, bias=c_bias[:, 0:1], scale=THIRD_ROOT)
                    nc.scalar.activation(t_l, t_e, ACT.Relu, bias=c_bias[:, 1:2]).then_inc(softplus_step, 1)
                    act.wait_ge(softplus_step, n + 3)
                    nc.scalar.activation(t_l, t_l, ACT.Ln, bias=c_bias[:, 2:3]).then_inc(softplus_parts, 1)

            def spread(when, k, i):
                if i in POOL_PAIRS:
                    act.wait_ge(pool_drive_made, CT * POOL_TILE * k + POOL_PAIRS.index(i) + 1)
                else:
                    act.wait_ge(drive_made, CT * OWN_TILE * k + OWN_PAIRS.index(i) + 1)
                bank, done = wait_filled(act, when, "SPREAD", 4 * i)
                nc.scalar.activation(Bs[:, 2 * i, :], bank[:, :], ACT.Copy).then_inc(done, 1)
                bank, done = wait_filled(act, when, "SPREAD", 4 * i + 1)
                nc.scalar.activation(Bs[:, 2 * i + 1, :], bank[:, :], ACT.Copy).then_inc(done, 1)
                act.wait_ge(weighted, STEPS * k + i + 1)
                bank, done = wait_filled(act, when, "SPREAD", 4 * i + 2)
                nc.scalar.activation(Cs[:, 2 * i, :], bank[:, :], ACT.Copy).then_inc(done, 1)
                bank, done = wait_filled(act, when, "SPREAD", 4 * i + 3)
                nc.scalar.activation(Cs[:, 2 * i + 1, :], bank[:, :], ACT.Copy).then_inc(done, 1)

            def decays(b, s):
                tile, pair = divmod(s, PAIRS)
                if pair == 0:
                    act.wait_ge(delta_made, CT * b + tile + 1)
                act.wait_ge(scanned, STEPS * b + s + 1)
                for j in range(2):
                    n = 2 * pair + j
                    last = nc.scalar.activation(decay[:, s % RING, j, 1:L], DELTA[:, tile, 1:L], ACT.Exp,
                                                scale=negA[:, tile, n:n + 1])
                last.then_inc(decay_made, 1)

            act.wait_ge(weights_in, 16 * 13)
            act.preload_act_table_set(TABLES)
            nc.scalar.activation(choose[:, :], pick_in[:, :], ACT.Copy).then_inc(a_made, 1)
            nc.scalar.activation(negA[:, :, :], negA[:, :, :], ACT.Exp).then_inc(a_made, 1)
            act.wait_ge(a_made, 2)
            nc.scalar.activation(negA[:, :, :], negA[:, :, :], ACT.Copy, scale=-1.0).then_inc(a_made, 1)
            act.wait_ge(a_made, 3)
            act.wait_ge(consts_made, 3)
            act.wait_ge(ints_made, 4)
            for name, i in first_order:
                if name == "UP" and i == 0:
                    stage((None, 0), "FFNSILU", 0, 0, True)
                if name == "XP":
                    stage((None, 0), "SILU", 0, 0, True)
                if name not in ("UP", "DOWN", "SPREAD"):
                    stage((None, 0), name, i, 0, True)
                if name == "XP":
                    stage((None, 0), "MID", 0, 0, True)
                    stage((None, 0), "LOW", 0, 0, True)
            with act.Fori(0, NB) as b:
                for s in range(STEPS):
                    for name, i in ACT_SLOTS.get(s, []):
                        if name == "SPREAD":
                            spread((b, 1) if i < AHEAD else (b, 0), b, i)
                    decays(b, s)
                    slot = ACT_SLOTS.get(s, [])
                    for place, (name, i) in enumerate(slot):
                        if name == "XC3":
                            act.wait_ge(u_made, b + 1)
                            act.wait_ge(summed, RING + STEPS * b - (PAIRS - SKIP_PAIR - 1))
                            nc.scalar.activation(XC[:, CT - 1, :], late_u, ACT.Copy).then_inc(u_moved, 1)
                        elif name == "ZCOPY":
                            act.wait_ge(z_silu_made, b + 1)
                            act.wait_ge(gated, CT * b + 1)
                            nc.scalar.activation(Z[:, 2:4, :], Zlate, ACT.Copy).then_inc(z_made, 1)
                        elif name == "TURN":
                            copy_out((b, 0), "TURN", i, YGT[:, i, :])
                        elif name != "SPREAD":
                            silu_next = slot[place + 1:place + 2] in ([("SILU", 0)], [("FFNSILU", 0)])
                            stage((b, 0), name, i, b if (name, i) == ("DT", CT - 1) else b + 1, silu_next=silu_next)
            for i in range(AHEAD):
                spread((NB, 1), NB, i)
            copy_out(("end", 0), "TURN", CT - 1, YGT[:, CT - 1, :])

        @block.vector
        def _(dve):
            def stage(when, name, i, k, first=False):
                if name == "STATS":
                    dve.wait_ge(x_in, 16 * k + 16)
                    for t in range(TT):
                        last = nc.vector.bn_stats(stats[:, t, :], X[:, t, :])
                    last.then_inc(stats_seen, 1)
                    dve.wait_ge(stats_seen, 2 * k + 1)
                    nc.vector.memset(spare[:, 0:1], 0.0)
                    for t in range(TT):
                        last = nc.vector.bn_aggr(moments[:, t, :], stats[:, t, :])
                    last.then_inc(moments_made, 1)
                elif name == "XN":
                    if not first:
                        dve.wait_ge(z_made, 1 + k)
                    dve.wait_ge(rstd_made, 2 * k + 1)
                    for t in range(TT):
                        last = nc.vector.tensor_scalar(XN[:, t, :], X[:, t, :], moments[:, t, 0:1], rstd[:, 0, t:t + 1],
                                                       ALU.subtract, ALU.mult)
                    last.then_inc(xn_made, 1)
                    dve.wait_ge(xn_made, k + 1)
                    for t in range(TT):
                        last = nc.vector.bn_stats(stats[:, t, :], XN[:, t, :])
                    last.then_inc(stats_seen, 1)
                    dve.wait_ge(stats_seen, 2 * k + 2)
                    nc.vector.memset(spare[:, 0:1], 0.0)
                    for t in range(TT):
                        last = nc.vector.bn_aggr(moments[:, t, :], stats[:, t, :])
                    last.then_inc(moments_made, 1)
                elif name == "XN2":
                    dve.wait_ge(rstd_made, 2 * k + 2)
                    dve.wait_ge(sum_made, k + 1)
                    bank, n = at_fill(when, "LN", KD - 1)
                    dve.wait_ge(filled[bank], n)
                    for t in range(TT):
                        last = nc.vector.tensor_scalar(XN[:, t, :], XN[:, t, :], moments[:, t, 0:1], rstd[:, 1, t:t + 1],
                                                       ALU.subtract, ALU.mult)
                    last.then_inc(xh_made, 1)
                elif name == "XI":
                    bank, done = wait_filled(dve, when, name, i)
                    dve.wait_ge(conv_scaled, CT * k + i + 1)
                    for j in range(1, K):
                        if j > 1:
                            dve.wait_ge(conv_step, 2 * (CT * k + i) + j - 1)
                        nc.vector.scalar_tensor_tensor(
                            out=CPRE[:, i, j:L], in0=bank[:, 0:L - j], scalar=taps[:, i, K - 1 - j:K - j],
                            in1=CPRE[:, i, j:L], op0=ALU.mult, op1=ALU.add,
                        ).then_inc(done if j == K - 1 else conv_step, 1)
                elif name == "UP":
                    if i == 0:
                        dve.wait_ge(silu_gate_made, k + 1)
                    bank, done = wait_filled(dve, when, name, i)
                    nc.vector.tensor_tensor(HG[:, i, :], bank[:, :], HG[:, i, :], ALU.mult).then_inc(done, 1)
                elif name == "DOWN":
                    if i == 0:
                        dve.wait_ge(sum_made, k + 1)
                    bank, done = wait_filled(dve, when, name, i)
                    x_part = X[:, 2 * i:2 * i + 2, :].rearrange("p t d -> p (t d)")
                    nc.vector.tensor_tensor(x_part, bank[:, :], x_part, ALU.add).then_inc(done, 1)
                elif name == "XP":
                    dve.wait_ge(high_made, k + 1)
                    bank, done = wait_filled(dve, when, name, 0)
                    nc.vector.tensor_tensor(rest[0:96, :], bank[0:96, :], pieces[:, :], ALU.subtract).then_inc(done, 1)
                elif name == "LOW":
                    dve.wait_ge(mid_made, k + 1)
                    nc.vector.tensor_tensor(rest[64:96, :], rest[64:96, :], mid_low, ALU.subtract).then_inc(rest_made, 1)
                elif name == "DT":
                    n = CT * k + i
                    dve.wait_ge(softplus_parts, n + 1)
                    nc.vector.scalar_tensor_tensor(out=t_u, in0=t_u, scalar=13.0 / 16.0, in1=t_e,
                                                   op0=ALU.add, op1=ALU.mult).then_inc(delta_step, 1)
                    dve.wait_ge(delta_step, 2 * n + 1)
                    nc.vector.tensor_tensor(t_u, t_u, t_l, ALU.min).then_inc(delta_step, 1)

            def gate_y(i, summed_count, z_count, b, late):
                bank, n = at_fill((b, late), "TURN", (i - 1) % CT)
                dve.wait_ge(filled[bank], n)
                dve.wait_ge(summed, summed_count)
                dve.wait_ge(z_made, 1 + z_count)
                nc.vector.tensor_tensor(turnbuf[:, :], yT[:, :], Z[:, i, :], ALU.mult).then_inc(gated, 1)

            def finish(when, b, i):
                if i == 0:
                    dve.wait_ge(reloaded, 16 * b + 16)
                bank, done = wait_filled(dve, when, "OUT", i)
                res = RES[:, 2 * i:2 * i + 2, :].rearrange("p t d -> p (t d)")
                nc.vector.tensor_tensor(res, bank[:, :], res, ALU.add).then_inc(done, 1)

            def start_tile(b, tile):
                dve.wait_ge(delta_made, CT * b + tile + 1)
                dve.wait_ge(u_moved, b + 1)
                dve.wait_ge(drive_made, OWN_TILE * (CT * b + tile + 1))
                nc.vector.tensor_tensor(du[:, 0, :], DELTA[:, tile, :], XC[:, tile, :], ALU.mult).then_inc(du_made, 1)

            def drives(b, s):
                tile, pair = divmod(s, PAIRS)
                if pair == 0:
                    start_tile(b, tile)
                    dve.wait_ge(du_made, CT * b + tile + 1)
                if tile == 0 and pair in OWN_PAIRS:
                    for j in (0, 1):
                        wait_drained(dve, (b, 1) if pair < AHEAD else (b, 0), "SPREAD", 4 * pair + j)
                if pair in POOL_PAIRS:
                    return
                dve.wait_ge(scanned, RING + STEPS * b + s - 1)
                nc.vector.tensor_tensor(drive[:, s % 2, :, :], du[:, :, :].to_broadcast([P, 2, L]),
                                        Bs[:, 2 * pair:2 * pair + 2, :], ALU.mult).then_inc(drive_made, 1)
                if pair == 0:
                    dve.wait_ge(pool_drive_made, POOL_TILE * (CT * b + tile + 1))
                    nc.vector.tensor_tensor(du_copy[:, 0, :], DELTA[:, tile, :], XC[:, tile, :],
                                            ALU.mult).then_inc(du_copied, 1)

            def scan(b, s):
                tile, pair = divmod(s, PAIRS)
                if pair in POOL_PAIRS:
                    dve.wait_ge(pool_drive_made, POOL_TILE * (CT * b + tile + 1) + POOL_PAIRS.index(pair) + 1)
                    driven = h[:, s % RING, :, :]
                else:
                    dve.wait_ge(drive_made, OWN_TILE * (CT * b + tile + 1) + OWN_PAIRS.index(pair) + 1)
                    driven = drive[:, s % 2, :, :]
                dve.wait_ge(decay_made, 1 + STEPS * b + s + 1)
                dve.wait_ge(summed, STEPS * b + s + 1)
                nc.vector.tensor_tensor_scan(
                    h[:, s % RING, :, :].rearrange("p a b -> p (a b)"),
                    decay[:, s % RING, :, :].rearrange("p a b -> p (a b)"),
                    driven.rearrange("p a b -> p (a b)"), 0.0, ALU.mult, ALU.add).then_inc(scanned, 1)

            nc.vector.memset(decay[:, :, :, 0:1], 0.0).then_inc(scanned, RING)
            nc.vector.memset(c_bias[:, 0:1], -0.75 * THIRD_ROOT).then_inc(consts_made, 1)
            nc.vector.memset(c_bias[:, 1:2], -SMALL).then_inc(z_made, 1)
            nc.vector.memset(c_bias[:, 2:3], 1.0 + SMALL).then_inc(consts_made, 1)
            nc.vector.memset(yT[:, :], 0.0).then_inc(summed, RING)
            nc.vector.memset(Z[:, CT - 1, :], 0.0).then_inc(drive_made, OWN_TILE)
            nc.vector.memset(spare[:, 1:2], 0.0).then_inc(decay_made, 1)
            nc.vector.memset(spare[:, 2:3], 0.0).then_inc(reloaded, 16)
            nc.vector.memset(spare[:, 3:4], 0.0).then_inc(stored, 16)
            dve.wait_ge(weights_in, 16 * 13)
            for c in range(CT):
                last = nc.vector.tensor_scalar(SKIP[:, c, :], eye[:, :], skip[:, c:c + 1], None, ALU.mult)
            last.then_inc(ints_made, 1)
            dve.wait_ge(ints_in, 48)
            for source, weight in ((HG[:, 0:3, :], W_g), (HG[:, 3:6, :], W_u), (CPRE[:, 0:3, :], W_d)):
                nc.vector.tensor_scalar(weight[:, :, :].rearrange("p k n -> p (k n)"),
                                        source.bitcast(I32).rearrange("p a b -> p (a b)"),
                                        QUANT, None, ALU.mult).then_inc(ints_made, 1)
            stage((None, 0), "STATS", 0, 0, True)
            stage((None, 0), "XN", 0, 0, True)
            stage((None, 0), "XN2", 0, 0, True)
            for name, i in first_order:
                if name in ("XI", "UP", "DOWN", "XP", "DT"):
                    stage((None, 0), name, i, 0, True)
                if name == "XP":
                    stage((None, 0), "LOW", 0, 0, True)
            with dve.Fori(0, NB) as b:
                drives(b, 0)
                for s in range(STEPS):
                    tile, pair = divmod(s, PAIRS)
                    if s + 1 < STEPS:
                        drives(b, s + 1)
                    scan(b, s)
                    for name, i in DVE_SLOTS.get(s, []):
                        if name == "YGATE":
                            before = i == CT - 1
                            gate_y(i, RING + STEPS * b + (0 if before else PAIRS * (i + 1)), b if before else b + 1, b, before)
                        elif name == "OUT":
                            finish((b, 0), b, i)
                        else:
                            stage((b, 0), name, i, b if (name, i) == ("DT", CT - 1) else b + 1)
            gate_y(CT - 1, RING + STEPS * NB, NB, NB, True)
            finish(("end", 0), NB, 0)
            finish(("end", 0), NB, 1)

        @block.gpsimd
        def _(pool):
            def stage(name, i, k):
                if name == "RSTD":
                    pool.wait_ge(moments_made, 2 * k + i + 1)
                    nc.gpsimd.tensor_tensor(rstd[:, i, :], moments[:, :, 1], c_eps[:, TT:2 * TT], ALU.add).then_inc(pow_step, 1)
                    pool.wait_ge(pow_step, 2 * k + i + 1)
                    nc.gpsimd.tensor_tensor(rstd[:, i, :], rstd[:, i, :], c_eps[:, 0:TT], ALU.pow).then_inc(rstd_made, 1)
                elif name == "DT":
                    n = CT * k + i
                    pool.wait_ge(delta_step, 2 * n + 2)
                    nc.gpsimd.tensor_tensor(DELTA[:, i, :], DELTA[:, i, :], t_u, ALU.add).then_inc(delta_made, 1)
                else:
                    pool.wait_ge(xn_made, k + 1)
                    nc.gpsimd.tensor_tensor(X[:, :, :], X[:, :, :], XN[:, :, :], ALU.add).then_inc(sum_made, 1)

            def weigh(b, s):
                pair = s % PAIRS
                pool.wait_ge(scanned, RING + STEPS * b + s + 1)
                if s < PAIRS:
                    for j in (2, 3):
                        wait_drained(pool, (b, 1) if pair < AHEAD else (b, 0), "SPREAD", 4 * pair + j)
                hs = h[:, s % RING, :, :]
                nc.gpsimd.tensor_tensor(hs, hs, Cs[:, 2 * pair:2 * pair + 2, :], ALU.mult).then_inc(weighted, 1)

            def pool_drive(b, s):
                tile, pair = divmod(s, PAIRS)
                pool.wait_ge(du_copied, CT * b + tile + 1)
                if tile == 0:
                    for j in (0, 1):
                        wait_drained(pool, (b, 1) if pair < AHEAD else (b, 0), "SPREAD", 4 * pair + j)
                pool.wait_ge(summed, STEPS * b + s + 1)
                nc.gpsimd.tensor_tensor(h[:, s % RING, :, :], du_copy[:, :, :].to_broadcast([P, 2, L]),
                                        Bs[:, 2 * pair:2 * pair + 2, :], ALU.mult).then_inc(pool_drive_made, 1)

            nc.gpsimd.memset(c_eps[:, TT:2 * TT], EPS).then_inc(pool_drive_made, POOL_TILE)
            nc.gpsimd.memset(c_eps[:, 0:TT], -0.5).then_inc(weighted, PAIRS)
            nc.gpsimd.memset(YGT[:, 0:CT - 1, :], 0.0).then_inc(consts_made, 1)
            pool.wait_ge(weighted, PAIRS)
            stage("RSTD", 0, 0)
            stage("RSTD", 1, 0)
            stage("SUM", 0, 0)
            for i in range(CT - 1):
                stage("DT", i, 0)
            with pool.Fori(0, NB) as b:
                for s in range(STEPS):
                    weigh(b, s)
                    if s + LEAD < STEPS and (s + LEAD) % PAIRS in POOL_PAIRS:
                        pool_drive(b, s + LEAD)
                    for name, i in POOL_SLOTS.get(s, []):
                        stage(name, i, b if (name, i) == ("DT", CT - 1) else b + 1)


def _laid_out(i):
    import numpy as np

    def columns(v):
        return np.ascontiguousarray(np.asarray(v).reshape(-1, P).T)

    def tiles(m):
        return np.ascontiguousarray(np.asarray(m).reshape(-1, P, m.shape[-1]).transpose(1, 0, 2))

    w_xp = np.asarray(i["L0_attn_W_xp"])
    rank = i["L0_attn_W_dt"].shape[0]
    w_bc, w_low = w_xp[:, rank:], w_xp[:, :rank]
    n2 = w_bc.shape[1]
    pick = np.tile(np.eye(n2, dtype=np.float32), (3, 1))
    return {
        "x": np.asarray(i["L0_attn_x"]),
        "ln_g": columns(i["L0_attn_ln_g"]),
        "ln_b": columns(i["L0_attn_ln_b"]),
        "w_in": np.asarray(i["L0_attn_W_in"]),
        "conv_w": tiles(np.asarray(i["L0_attn_conv_w"])[:, 0, :]),
        "conv_b": columns(i["L0_attn_conv_b"]),
        "w_xp": np.concatenate([w_bc, w_bc, w_bc, w_low], axis=1),
        "w_dt": np.asarray(i["L0_attn_W_dt"]),
        "dt_bias": columns(i["L0_attn_dt_bias"]),
        "a_log": tiles(np.asarray(i["L0_attn_A_log"])),
        "d_skip": columns(i["L0_attn_D_skip"]),
        "w_out": np.asarray(i["L0_attn_W_out"]),
        "w_gate": np.ascontiguousarray(np.asarray(i["L0_ffn_w_gate"]).T),
        "w_up": np.ascontiguousarray(np.asarray(i["L0_ffn_w_up"]).T),
        "w_down": np.ascontiguousarray(np.asarray(i["L0_ffn_w_down"]).T),
        "ident": np.eye(P, dtype=np.float32),
        "pick": pick,
    }


def kernel(**inputs):
    import numpy as _np
    import concourse.bacc as _bacc
    from concourse.bass_utils import run_bass_kernel_spmd as _run

    nc = _bacc.Bacc("TRN2", target_bir_lowering=False, num_devices=1)
    arrays, args = {}, []
    for name, a in _laid_out(inputs).items():
        arrays[f"in_{name}"] = a
        args.append(nc.dram_tensor(f"in_{name}", a.shape, mybir.dt.from_np(a.dtype), kind="ExternalInput").ap())
    shape = arrays["in_x"].shape
    args.append(nc.dram_tensor("out_dram", shape, F32, kind="ExternalOutput").ap())
    bass_mamba_ffn_block_kernel(nc, *args)
    r = _run(nc, [arrays], core_ids=[0])
    return r.results[0]["out_dram"]
```
